# Optimizing a Trainium2 kernel written in Bass

```python
import numpy as np
import jax
import jax.numpy as jnp

def _softmax(x, axis=-1):
    return jax.nn.softmax(x, axis=axis)

def _gelu(x):
    return jax.nn.gelu(x, approximate=True)

def _silu(x):
    return jax.nn.silu(x)

def _sigmoid(x):
    return jax.nn.sigmoid(x)

def _layernorm(x, axis=-1, eps=1e-05):
    m = jnp.mean(x, axis=axis, keepdims=True)
    v = jnp.var(x, axis=axis, keepdims=True)
    return (x - m) / jnp.sqrt(v + eps)

def _scatter_add(tgt, idx, src, axis=0):
    return tgt.at[idx].add(src)

def _segment_sum(src, seg, n):
    return jax.ops.segment_sum(src, seg, n)
kernel_name = 'mk_xattn_ffn_d1_seqx_r2_e8ff2b'

def setup_inputs(seed: int=0):
    np.random.seed(seed)
    _w = jnp.asarray

    def _rec_inputs():
        import jax
        import jax.numpy as jnp
        _rk = jax.random.key(seed)
        x = -0.0002928 + 1 * jax.random.normal(jax.random.fold_in(_rk, 1), (2, 2048, 512), jnp.float32)
        _lenS = 2048 - jax.random.randint(jax.random.fold_in(_rk, 7), (2,), 0, max(1, 2048 // 4) + 1, jnp.int32)
        _lenS2 = 77 - jax.random.randint(jax.random.fold_in(_rk, 8), (2,), 0, max(1, 77 // 4) + 1, jnp.int32)
        _ctx_768P = jax.random.normal(jax.random.fold_in(_rk, 11), (2, 16, 384), jnp.float32)
        _ctx_768c = jax.random.dirichlet(jax.random.fold_in(_rk, 511), 0.3 * jnp.ones((16,), jnp.float32), (2, 77))
        _ctx_768t = jnp.einsum('bsk,bkd->bsd', _ctx_768c, _ctx_768P)
        _ctx_768t = _ctx_768t * jax.lax.rsqrt(jnp.mean(jnp.square(_ctx_768t)) + 1e-12) * 0.953939
        ctx_768 = 2.09791e-05 + 1.00001 * (_ctx_768t + 0.3 * jax.random.normal(jax.random.fold_in(_rk, 611), (2, 77, 384), jnp.float32))
        return (x, ctx_768)
    x, ctx_768 = _rec_inputs()

    def _L0_xattn_setup():
        import jax, jax.numpy as jnp
        import numpy as np
        HEADS = 8
        DIM_HEAD = 128
        ATTN_MATRIX_SCALE = 1.5
        SCALE = DIM_HEAD ** (-0.5)

        def _split_heads(t):
            b, n, _ = t.shape
            t = t.reshape(b, n, HEADS, DIM_HEAD)
            return t.transpose(2, 0, 1, 3).reshape(HEADS, b * n, DIM_HEAD)
        key = jax.random.key(seed)
        ks = jax.random.split(key, 7)
        b, n, m = (2, 1024, 1024)
        qd, cd, inner = (512, 384, HEADS * DIM_HEAD)
        x = jax.random.normal(ks[0], (b, n, qd), dtype=jnp.float32)
        context = jax.random.normal(ks[1], (b, m, cd), dtype=jnp.float32)
        Wq = jax.random.normal(ks[2], (qd, inner), dtype=jnp.float32) * qd ** (-0.5)
        Wk = jax.random.normal(ks[3], (cd, inner), dtype=jnp.float32) * cd ** (-0.5)
        Wv = jax.random.normal(ks[4], (cd, inner), dtype=jnp.float32) * cd ** (-0.5)
        Wout = jax.random.normal(ks[5], (inner, qd), dtype=jnp.float32) * inner ** (-0.5)
        bout = jnp.zeros((qd,), dtype=jnp.float32)
        return {'x': x, 'context': context, 'Wq': Wq, 'Wk': Wk, 'Wv': Wv, 'Wout': Wout, 'bout': bout}
    _L0_xattn_all = _L0_xattn_setup()
    _L0_xattn_in = {k: v for k, v in _L0_xattn_all.items() if k in ('Wq', 'Wk', 'Wv', 'Wout', 'bout')}
    del _L0_xattn_all

    def _L0_ffn_setup():
        import jax, jax.numpy as jnp
        import numpy as np
        DIM = 512

        def _reference_tuple_inner(x, W_r, W_k, W_v, mu_r, mu_k):
            B, T, C = x.shape
            x_prev = jnp.concatenate([jnp.zeros((B, 1, C), x.dtype), x[:, :-1, :]], axis=1)
            xr = mu_r * x + (1.0 - mu_r) * x_prev
            xk = mu_k * x + (1.0 - mu_k) * x_prev
            r = jax.nn.sigmoid(jnp.einsum('btc,dc->btd', xr, W_r))
            k = jnp.einsum('btc,dc->btd', xk, W_k)
            k_act = jnp.square(jax.nn.relu(k))
            out = r * jnp.einsum('btc,dc->btd', k_act, W_v)
            new_state = x[:, -1, :]
            return (out, new_state)
        key = jax.random.key(seed)
        ks = jax.random.split(key, 6)
        B, T, C = (8, 1024, DIM)
        x = jax.random.normal(ks[0], (B, T, C), dtype=jnp.float32)
        s = 1.0 / np.sqrt(C)
        W_r = jax.random.uniform(ks[1], (C, C), jnp.float32, -s, s)
        W_k = jax.random.uniform(ks[2], (C, C), jnp.float32, -s, s)
        W_v = jax.random.uniform(ks[3], (C, C), jnp.float32, -s, s)
        mu_r = jax.random.uniform(ks[4], (C,), jnp.float32)
        mu_k = jax.random.uniform(ks[5], (C,), jnp.float32)
        return {'x': x, 'W_r': W_r, 'W_k': W_k, 'W_v': W_v, 'mu_r': mu_r, 'mu_k': mu_k}
    _L0_ffn_all = _L0_ffn_setup()
    _L0_ffn_in = {k: v for k, v in _L0_ffn_all.items() if k in ('W_r', 'W_k', 'W_v', 'mu_r', 'mu_k')}
    del _L0_ffn_all
    return {'x': x, 'ctx_768': ctx_768, 'L0_xattn_Wq': _L0_xattn_in['Wq'], 'L0_xattn_Wk': _L0_xattn_in['Wk'], 'L0_xattn_Wv': _L0_xattn_in['Wv'], 'L0_xattn_Wout': _L0_xattn_in['Wout'], 'L0_xattn_bout': _L0_xattn_in['bout'], 'L0_ffn_W_r': _L0_ffn_in['W_r'], 'L0_ffn_W_k': _L0_ffn_in['W_k'], 'L0_ffn_W_v': _L0_ffn_in['W_v'], 'L0_ffn_mu_r': _L0_ffn_in['mu_r'], 'L0_ffn_mu_k': _L0_ffn_in['mu_k']}

def reference(x, ctx_768, L0_xattn_Wq, L0_xattn_Wk, L0_xattn_Wv, L0_xattn_Wout, L0_xattn_bout, L0_ffn_W_r, L0_ffn_W_k, L0_ffn_W_v, L0_ffn_mu_r, L0_ffn_mu_k):
    import jax
    import jax.numpy as jnp

    def _L0_xattn_ref(x, context, Wq, Wk, Wv, Wout, bout):
        import jax, jax.numpy as jnp
        import numpy as np
        HEADS = 8
        DIM_HEAD = 128
        ATTN_MATRIX_SCALE = 1.5
        SCALE = DIM_HEAD ** (-0.5)

        def _split_heads(t):
            b, n, _ = t.shape
            t = t.reshape(b, n, HEADS, DIM_HEAD)
            return t.transpose(2, 0, 1, 3).reshape(HEADS, b * n, DIM_HEAD)
        b, n, _ = x.shape
        qh = _split_heads(jnp.einsum('bnq,qi->bni', x, Wq))
        kh = _split_heads(jnp.einsum('bmc,ci->bmi', context, Wk))
        vh = _split_heads(jnp.einsum('bmc,ci->bmi', context, Wv))
        sim = jnp.einsum('hid,hjd->hij', qh, kh) * SCALE
        mean = jnp.mean(sim, axis=-1, keepdims=True)
        sim = (sim - mean) * ATTN_MATRIX_SCALE + mean
        attn = jax.nn.softmax(sim, axis=-1)
        out = jnp.einsum('hij,hjd->hid', attn, vh)
        out = out.reshape(HEADS, b, n, DIM_HEAD).transpose(1, 2, 0, 3)
        out = out.reshape(b, n, HEADS * DIM_HEAD)
        return jnp.einsum('bni,iq->bnq', out, Wout) + bout

    def _L0_ffn_ref(x, W_r, W_k, W_v, mu_r, mu_k):
        import jax, jax.numpy as jnp
        import numpy as np
        DIM = 512

        def _reference_tuple_inner(x, W_r, W_k, W_v, mu_r, mu_k):
            B, T, C = x.shape
            x_prev = jnp.concatenate([jnp.zeros((B, 1, C), x.dtype), x[:, :-1, :]], axis=1)
            xr = mu_r * x + (1.0 - mu_r) * x_prev
            xk = mu_k * x + (1.0 - mu_k) * x_prev
            r = jax.nn.sigmoid(jnp.einsum('btc,dc->btd', xr, W_r))
            k = jnp.einsum('btc,dc->btd', xk, W_k)
            k_act = jnp.square(jax.nn.relu(k))
            out = r * jnp.einsum('btc,dc->btd', k_act, W_v)
            new_state = x[:, -1, :]
            return (out, new_state)
        return _reference_tuple_inner(x, W_r, W_k, W_v, mu_r, mu_k)[0]
    x = x + _L0_xattn_ref(_layernorm(x, axis=-1), ctx_768, L0_xattn_Wq, L0_xattn_Wk, L0_xattn_Wv, L0_xattn_Wout, L0_xattn_bout)
    x = x + _L0_ffn_ref(_layernorm(x, axis=-1), L0_ffn_W_r, L0_ffn_W_k, L0_ffn_W_v, L0_ffn_mu_r, L0_ffn_mu_k)
    return x

_drawn_inputs = setup_inputs


def setup_inputs(seed=0):
    import zlib

    import numpy as np

    out = dict(_drawn_inputs(seed))
    spreads = {'L0_xattn_bout': (0.0, 0.1)}
    factors = {'L0_ffn_W_r': 3.351, 'L0_ffn_mu_r': 7.54}
    for name, (base, spread) in spreads.items():
        noise = np.random.default_rng([zlib.crc32(name.encode()), seed]).standard_normal(out[name].shape)
        drawn = base * np.exp(spread * noise) if base else spread * noise
        out[name] = jnp.asarray(drawn.astype(out[name].dtype))
    for name, factor in factors.items():
        out[name] = (out[name] * factor).astype(out[name].dtype)
    return out
```

```python
from contextlib import ExitStack

import concourse.bass as bass
from concourse import mybir

F32 = mybir.dt.float32
F32R = mybir.dt.float32r
ALU = mybir.AluOpType
ACT = mybir.ActivationFunctionType
X = mybir.AxisListType.X

P = 128
HEADS = 8
STRETCH = 1.5
EPS = 1e-5
BANK = 512


def xattn_ffn(nc, x, ctx_768, Wq, Wk, Wv, Wout, bout, W_r, W_k, W_v, mu_r, mu_k, out):
    batches, seq, D = x.shape
    C = ctx_768.shape[2]
    J = ctx_768.shape[0] * ctx_768.shape[1]
    inner = Wq.shape[1]
    DH = inner // HEADS
    assert DH == P and D == 4 * P and C % P == 0 and P < J < 2 * P

    DC = D // P
    CC = C // P
    HJ = HEADS * J
    MC = -(-(HJ + 1) // P)
    LAST = HJ + 1 - (MC - 1) * P
    TILES = batches * seq // P
    GROUP = 4
    GROUPS = TILES // GROUP
    PAIRS = TILES // 2
    GROUPS_PER_BATCH = seq // P // GROUP
    HPB = BANK // J
    HEAD_BANKS = [(b, min(b + HPB, HEADS)) for b in range(0, HEADS, HPB)]
    PT_BANKS = [(c, min(c + 4, MC)) for c in range(0, MC, 4)]
    assert len(HEAD_BANKS) == 3 and len(PT_BANKS) == 3 and GROUPS_PER_BATCH == 4
    SCALE = float(DH) ** -0.5

    SEGMENTS = [(m, h, max(m * P, h * J), min((m + 1) * P, (h + 1) * J))
                for m in range(MC) for h in range(HEADS)
                if max(m * P, h * J) < min((m + 1) * P, (h + 1) * J)]

    xt = x.rearrange("b s d -> (b s) d")
    yt = out.rearrange("b s d -> (b s) d")
    ctx_rows = ctx_768.rearrange("b s d -> (b s) d")

    with ExitStack() as stack:
        base = -(-nc.sbuf_base // 64) * 64
        cursor = [base]

        def size_of(shape):
            n = 4
            for s in shape[1:]:
                n *= s
            return -(-n // 32) * 32

        def sb(name, shape, dt=F32, at=None):
            offset = cursor[0] if at is None else at
            if at is None:
                cursor[0] += size_of(shape)
            return nc.alloc_sbuf_tensor_at(name, shape, dt, offset=offset)

        A_hi = sb("A_hi", [P, DC, HJ], F32R)
        A_lo = sb("A_lo", [P, DC, HJ], F32R)
        B_hi = sb("B_hi", [P, MC, D], F32R)
        B_lo = sb("B_lo", [P, MC, D], F32R)
        at_ffn_weights = cursor[0]
        WT = {}
        for w in ("k", "r", "v"):
            WT[w] = (sb(f"W{w}T_hi", [P, DC, D], F32R), sb(f"W{w}T_lo", [P, DC, D], F32R))
        x_in = [sb(f"x_in{i}", [P, D]) for i in range(4)]
        xn = sb("xn", [P, D])
        at_xn2 = cursor[0]
        xn2 = sb("xn2", [P, D])
        xT_hi = sb("xT_hi", [P, DC, P], F32R)
        xT_lo = sb("xT_lo", [P, DC, P], F32R)
        probs = sb("probs", [P, MC * P])
        at_pT = cursor[0]
        pT_hi = sb("pT_hi", [P, MC, P], F32R)
        pT_lo = sb("pT_lo", [P, MC, P], F32R)
        at_x2 = cursor[0]
        x2 = [sb(f"x2_{i}", [P, D]) for i in range(4)]
        at_xn2T = cursor[0]
        xn2T = sb("xn2T", [P, DC, 2 * P + 1])
        at_mix = cursor[0]
        xk_hi = sb("xk_hi", [P, DC, 2 * P], F32R)
        xk_lo = sb("xk_lo", [P, DC, 2 * P], F32R)
        xr_hi = sb("xr_hi", [P, DC, 2 * P], F32R)
        xr_lo = sb("xr_lo", [P, DC, 2 * P], F32R)
        xk = sb("xk", [P, DC, 2 * P])
        act_hi = sb("act_hi", [P, DC, 2 * P], F32R)
        act_lo = sb("act_lo", [P, DC, 2 * P], F32R)
        at_act = cursor[0]
        act = sb("act", [P, DC, 2 * P])
        xr = sb("xr", [P, DC, 2 * P], at=at_act)
        gate = [sb(f"gate{i}", [P, D]) for i in range(2)]
        identity = sb("identity", [P, P])
        onehot = sb("onehot", [1, P])
        mu = {"k": sb("mu_k_cols", [P, DC]), "r": sb("mu_r_cols", [P, DC])}
        one_minus_mu = {"k": sb("omu_k_cols", [P, DC]), "r": sb("omu_r_cols", [P, DC])}
        minus_half = sb("minus_half", [P, 1])
        halo = sb("halo", [P, DC, 4])
        raw1 = sb("raw1", [P, 6])
        stats1 = sb("stats1", [P, 2])
        var1 = sb("var1", [P, 1])
        rstd1 = sb("rstd1", [P, 1])
        raw2 = sb("raw2", [P, 6])
        stats2 = sb("stats2", [P, 2])
        var2 = sb("var2", [P, 1])
        rstd2 = sb("rstd2", [P, 1])
        neg_max = sb("neg_max", [P, HEADS])
        row_sum = sb("row_sum", [P, HEADS])
        inv_sum = sb("inv_sum", [P, HEADS])
        ctx_sum = sb("ctx_sum", [P, CC])
        ctx_shift = sb("ctx_shift", [P, CC])

        wq = sb("wq", [P, DC, inner], at=at_ffn_weights)
        wqT = sb("wqT", [P, HEADS, D], at=at_ffn_weights + size_of([P, DC, inner]))
        wk = sb("wk", [P, CC, inner], at=at_ffn_weights + 2 * size_of([P, DC, inner]))
        at = at_mix
        wv = sb("wv", [P, CC, inner], at=at)
        at += size_of([P, CC, inner])
        wout = sb("wout", [P, HEADS, D], at=at)
        at_raw_k = at + size_of([P, HEADS, D])
        raw_w = {"r": sb("raw_wr", [P, DC, D], at=at_mix),
                 "v": sb("raw_wv", [P, DC, D], at=at_mix + size_of([P, DC, D])),
                 "k": sb("raw_wk", [P, DC, D], at=at_raw_k)}
        vT_pad = sb("vT_pad", [P, len(SEGMENTS), P], at=at_pT)
        kT = sb("kT", [P, HEADS, J], at=at_x2)
        ctx0 = sb("ctx0", [P, C], at=at_x2 + size_of([P, HEADS, J]))
        ctx1 = sb("ctx1", [J - P, C], at=at_x2 + size_of([P, HEADS, J]) + size_of([P, C]))
        ctxT = sb("ctxT", [P, CC, J], at=at_xn2T)
        ctxT_keys = sb("ctxT_keys", [P, CC, J], at=at_xn2T + size_of([P, CC, J]))
        bout_row = sb("bout_row", [1, D], at=at_xn2)

        def bank(name):
            return stack.enter_context(nc.psum_tensor(name, [P, BANK], F32))

        S = [bank(f"scores{i}") for i in range(3)]
        T = [bank(f"turn{i}") for i in range(3)]
        O = bank("attended")
        XB = bank("turned_x")

        def sem(name):
            return stack.enter_context(nc.semaphore(name))

        ctx_loaded, wk_loaded, wq_loaded = sem("ctx_loaded"), sem("wk_loaded"), sem("wq_loaded")
        wv_loaded, wout_loaded, mu_loaded = sem("wv_loaded"), sem("wout_loaded"), sem("mu_loaded")
        ffn_loaded = {w: sem(f"ffn_{w}_loaded") for w in "krv"}
        x_loaded = [sem(f"x_loaded{i}") for i in range(4)]
        stored = [sem(f"stored{i}") for i in range(4)]
        identity_zeroed, identity_ready = sem("identity_zeroed"), sem("identity_ready")
        consts_ready, vT_pad_zeroed = sem("consts_ready"), sem("vT_pad_zeroed")
        ones_zeroed, mu_ready = sem("ones_zeroed"), sem("mu_ready")
        ctxT_turned, ctx_summed, ctx_shifted, ctxT_ready = (
            sem("ctxT_turned"), sem("ctx_summed"), sem("ctx_shifted"), sem("ctxT_ready"))
        keys_done, kT_ready = sem("keys_done"), sem("kT_ready")
        wq_turned, wqT_even, wqT_odd = sem("wq_turned"), sem("wqT_even"), sem("wqT_odd")
        A_done, A_hi_ready, A_ready = sem("A_done"), sem("A_hi_ready"), sem("A_ready")
        values_done, vT_act, vT_dve = sem("values_done"), sem("vT_act"), sem("vT_dve")
        B_done, B_hi_ready, B_ready = sem("B_done"), sem("B_hi_ready"), sem("B_ready")
        W_turned, W_hi_ready, W_ready = sem("W_turned"), sem("W_hi_ready"), sem("W_ready")
        raw1_ready, stats1_ready, var1_ready, rstd1_ready, xn_ready = (
            sem("raw1_ready"), sem("stats1_ready"), sem("var1_ready"), sem("rstd1_ready"), sem("xn_ready"))
        x_turned, xT_hi_ready, xT_ready = sem("x_turned"), sem("xT_hi_ready"), sem("xT_ready")
        scores_done = sem("scores_done")
        max_ready = sem("max_ready")
        exp_done, inv_ready, probs_ready = sem("exp_done"), sem("inv_ready"), sem("probs_ready")
        probs_turned, pT_hi_ready, pT_ready = (
            sem("probs_turned"), sem("pT_hi_ready"), sem("pT_ready"))
        attended, x2_ready = sem("attended"), sem("x2_ready")
        raw2_ready, stats2_ready, var2_ready, rstd2_ready, xn2_ready = (
            sem("raw2_ready"), sem("stats2_ready"), sem("var2_ready"), sem("rstd2_ready"), sem("xn2_ready"))
        x2_turned, xn2T_ready = sem("x2_turned"), sem("xn2T_ready")
        xk_scaled, xk_ready, xk_hi_ready, xk_split = (
            sem("xk_scaled"), sem("xk_ready"), sem("xk_hi_ready"), sem("xk_split"))
        xr_scaled, xr_ready, xr_hi_ready, xr_split = (
            sem("xr_scaled"), sem("xr_ready"), sem("xr_hi_ready"), sem("xr_split"))
        halo_kept, halo_ready = sem("halo_kept"), sem("halo_ready")
        k_done, relu_ready, square_ready, act_hi_ready, act_split = (
            sem("k_done"), sem("relu_ready"), sem("square_ready"), sem("act_hi_ready"), sem("act_split"))
        r_done, gate_ready, kv_done, gated, out_ready = (
            sem("r_done"), sem("gate_ready"), sem("kv_done"), sem("gated"), sem("out_ready"))

        def begun(n):
            return not isinstance(n, int) or n >= 0

        def is_tile(t):
            return not isinstance(t, int) or 0 <= t < TILES

        def is_pair(q):
            return not isinstance(q, int) or 0 <= q < PAIRS


        def place(g, s):
            return 4 * g + s, 2 * g + s // 2 - 1, s % 2

        def turns(eng, step):
            step(0, 2)
            step(0, 3)
            with eng.Fori(1, GROUPS - 1) as g:
                for s in range(GROUP):
                    step(g, s)
            for s in range(GROUP):
                step(GROUPS - 1, s)
            step(GROUPS, 0)
            step(GROUPS, 1)

        block = stack.enter_context(nc.Block())

        @block.sync
        def _(sp):
            sp.dma_start(ctx0[:], ctx_rows[0:P, :]).then_inc(ctx_loaded, 16)
            sp.dma_start(ctx1[:], ctx_rows[P:J, :]).then_inc(ctx_loaded, 16)
            sp.dma_start(wk[:], Wk.rearrange("(c p) n -> p c n", p=P)).then_inc(wk_loaded, 16)
            sp.dma_start(wq[:], Wq.rearrange("(c p) n -> p c n", p=P)).then_inc(wq_loaded, 16)
            for i in range(4):
                sp.dma_start(x_in[i][:], xt[i * P:(i + 1) * P, :]).then_inc(x_loaded[i], 16)
            sp.dma_start(wv[:], Wv.rearrange("(c p) n -> p c n", p=P)).then_inc(wv_loaded, 16)
            sp.dma_start(wout[:], Wout.rearrange("(h p) n -> p h n", p=P)).then_inc(wout_loaded, 16)
            sp.dma_start(bout_row[:], bout.rearrange("(a d) -> a d", a=1)).then_inc(wout_loaded, 16)
            with nc.allow_non_contiguous_dma(reason="two vectors of 512 as columns"):
                sp.dma_start(mu["k"][:], mu_k.rearrange("(c p) -> p c", p=P)).then_inc(mu_loaded, 16)
                sp.dma_start(mu["r"][:], mu_r.rearrange("(c p) -> p c", p=P)).then_inc(mu_loaded, 16)
            sp.dma_start(raw_w["k"][:], W_k.rearrange("(c p) n -> p c n", p=P)).then_inc(ffn_loaded["k"], 16)
            sp.wait_ge(values_done, 3)
            sp.wait_ge(B_done, MC)
            sp.dma_start(raw_w["r"][:], W_r.rearrange("(c p) n -> p c n", p=P)).then_inc(ffn_loaded["r"], 16)
            sp.dma_start(raw_w["v"][:], W_v.rearrange("(c p) n -> p c n", p=P)).then_inc(ffn_loaded["v"], 16)

            def step(g, s):
                t, q, half = place(g, s)
                if is_tile(t + 4) and is_tile(t):
                    sp.wait_ge(x2_ready, t + 1)
                    sp.dma_start(x_in[s][:], xt[bass.ds((t + 4) * P, P), :]).then_inc(x_loaded[s], 16)
                if is_pair(q) and half == 1:
                    for j in range(2):
                        slot = (s - 3 + j) % 4
                        sp.wait_ge(out_ready, 2 * q + j + 1)
                        sp.dma_start(yt[bass.ds((2 * q + j) * P, P), :], x2[slot][:]).then_inc(stored[slot], 16)

            step(0, 0)
            step(0, 1)
            turns(sp, step)
            for i in range(4):
                sp.wait_ge(stored[i], 16 * GROUPS)

        @block.tensor
        def _(te):
            def three_passes(psum, left, right, first, last):
                te.matmul(psum, left[0], right[0], start=first, stop=False)
                te.matmul(psum, left[0], right[1], start=False, stop=False)
                return te.matmul(psum, left[1], right[0], start=False, stop=last)

            def turn_x(t):
                te.wait_ge(xn_ready, t + 1)
                if begun(t - 3):
                    te.wait_ge(xn2T_ready, t - 2)
                for c in range(DC):
                    last = te.transpose(XB[:, c * P:(c + 1) * P], xn[:, c * P:(c + 1) * P], identity[:])
                last.then_inc(x_turned, 1)

            def scores(t):
                te.wait_ge(xT_ready, t + 1)
                if begun(t - 1):
                    te.wait_ge(exp_done, t)
                for b, (h0, h1) in enumerate(HEAD_BANKS):
                    n0, n1 = h0 * J, h1 * J
                    for c in range(DC):
                        last = three_passes(S[b][:, 0:n1 - n0], (xT_hi[:, c, :], xT_lo[:, c, :]),
                                            (A_hi[:, c, n0:n1], A_lo[:, c, n0:n1]), c == 0, c == DC - 1)
                    last.then_inc(scores_done, 1)

            def turn_probs(t, q, half):
                te.wait_ge(probs_ready, t + 1)
                for b, (c0, c1) in enumerate(PT_BANKS):
                    if half == 1 and is_pair(q):
                        if b < 2:
                            te.wait_ge(relu_ready, 2 * q + b + 1)
                        else:
                            te.wait_ge(gate_ready, 2 * q + 1)
                    if half == 0 and begun(q - 1):
                        if b == 0:
                            te.wait_ge(gate_ready, 2 * q)
                        else:
                            te.wait_ge(gated, 2 * q + b - 2)
                    for c in range(c0, c1):
                        last = te.transpose(T[b][:, (c - c0) * P:(c - c0 + 1) * P],
                                            probs[:, c * P:(c + 1) * P], identity[:])
                    last.then_inc(probs_turned, 1)

            def attend(t):
                if begun(t - 1):
                    te.wait_ge(x2_ready, t)
                for b, (c0, c1) in enumerate(PT_BANKS):
                    te.wait_ge(pT_ready, 3 * t + b + 1)
                    for c in range(c0, c1):
                        k = LAST if c == MC - 1 else P
                        last = three_passes(O[:], (pT_hi[0:k, c, :], pT_lo[0:k, c, :]),
                                            (B_hi[0:k, c, :], B_lo[0:k, c, :]), c == 0, c == MC - 1)
                last.then_inc(attended, 1)

            def ffn_rows(bank, parts, j, weights):
                for c in range(DC):
                    rows = tuple(p[:, c, j * P:(j + 1) * P] for p in parts)
                    last = three_passes(bank[:], rows, tuple(w[:, c, :] for w in weights), c == 0, c == DC - 1)
                return last

            def ffn_first(q):
                te.wait_ge(xk_split, q + 1)
                for j in range(2):
                    for m in (2 * j, 2 * j + 1):
                        for c in range(DC):
                            cols = tuple(w[:, c, m * P:(m + 1) * P] for w in WT["k"])
                            last = three_passes(T[j][:, (m % 2) * 2 * P:(m % 2 + 1) * 2 * P], cols,
                                                (xk_hi[:, c, :], xk_lo[:, c, :]), c == 0, c == DC - 1)
                    last.then_inc(k_done, 1)
                te.wait_ge(xr_split, q + 1)
                ffn_rows(T[2], (xr_hi, xr_lo), 0, WT["r"]).then_inc(r_done, 1)

            def ffn_second(q):
                ffn_rows(T[0], (xr_hi, xr_lo), 1, WT["r"]).then_inc(r_done, 1)
                te.wait_ge(act_split, 2 * q + 2)
                for j in range(2):
                    ffn_rows(T[1 + j], (act_hi, act_lo), j, WT["v"]).then_inc(kv_done, 1)

            def turn_x2(t):
                te.wait_ge(xn2_ready, t + 1)
                if is_tile(t + 2):
                    te.wait_ge(xT_ready, t + 3)
                elif begun(t - 1):
                    te.wait_ge(xn2T_ready, t)
                for c in range(DC):
                    last = te.transpose(XB[:, c * P:(c + 1) * P], xn2[:, c * P:(c + 1) * P], identity[:])
                last.then_inc(x2_turned, 1)

            def step(g, s):
                t, q, half = place(g, s)
                tail = not (is_tile(t) or is_tile(t + 1))
                if is_tile(t):
                    turn_probs(t, q, half)
                if is_tile(t + 1):
                    scores(t + 1)
                if is_tile(t):
                    attend(t)
                if is_tile(t + 2):
                    turn_x(t + 2)
                if is_pair(q):
                    if tail and half == 0:
                        te.wait_ge(gate_ready, 2 * q)
                        te.wait_ge(gated, 2 * q)
                    if tail and half == 1:
                        te.wait_ge(relu_ready, 2 * q + 2)
                        te.wait_ge(gate_ready, 2 * q + 1)
                    (ffn_second if half else ffn_first)(q)
                if is_tile(t):
                    turn_x2(t)

            te.wait_ge(identity_ready, 1)
            te.wait_ge(ctx_loaded, 32)
            for c in range(CC):
                te.transpose(XB[:, c * J:c * J + P], ctx0[:, c * P:(c + 1) * P], identity[:])
                last = te.transpose(XB[:, c * J + P:(c + 1) * J], ctx1[:, c * P:(c + 1) * P],
                                    identity[0:J - P, 0:J - P])
            last.then_inc(ctxT_turned, 1)

            te.wait_ge(wk_loaded, 16)
            te.wait_ge(ctxT_ready, 2)
            for b, (h0, h1) in enumerate(HEAD_BANKS):
                for h in range(h0, h1):
                    for c in range(CC):
                        last = te.matmul(S[b][:, (h - h0) * J:(h - h0 + 1) * J], wk[:, c, h * P:(h + 1) * P],
                                         ctxT_keys[:, c, :], start=(c == 0), stop=(c == CC - 1))
                last.then_inc(keys_done, 1)

            te.wait_ge(wq_loaded, 16)
            for h in range(HEADS):
                if h >= 4:
                    te.wait_ge(wqT_odd if h % 2 else wqT_even, (h - 4) // 2 + 1)
                to = (T + [O])[h % 4]
                for c in range(DC):
                    last = te.transpose(to[:, c * P:(c + 1) * P], wq[:, c, h * P:(h + 1) * P], identity[:])
                last.then_inc(wq_turned, 1)

            te.wait_ge(kT_ready, 3)
            te.wait_ge(wqT_even, HEADS // 2)
            te.wait_ge(wqT_odd, HEADS // 2)
            for c in range(DC):
                if c >= 2:
                    te.wait_ge(A_ready, 3 * (c - 1))
                for b, (h0, h1) in enumerate(HEAD_BANKS):
                    to = (T if c % 2 else S)[b]
                    for h in range(h0, h1):
                        last = te.matmul(to[:, (h - h0) * J:(h - h0 + 1) * J], wqT[:, h, c * P:(c + 1) * P],
                                         kT[:, h, :], start=True, stop=True)
                    last.then_inc(A_done, 1)

            turn_x(0)
            te.wait_ge(A_ready, 3 * DC)
            scores(0)
            turn_x(1)

            te.wait_ge(wv_loaded, 16)
            for b, (h0, h1) in enumerate(HEAD_BANKS):
                for h in range(h0, h1):
                    for c in range(CC):
                        last = te.matmul(T[b][:, (h - h0) * J:(h - h0 + 1) * J], wv[:, c, h * P:(h + 1) * P],
                                         ctxT[:, c, :], start=(c == 0), stop=(c == CC - 1))
                last.then_inc(values_done, 1)

            te.wait_ge(wout_loaded, 32)
            te.wait_ge(vT_act, 2)
            te.wait_ge(vT_dve, 1)
            for m in range(MC):
                if m >= 4:
                    te.wait_ge(B_ready, m - 3)
                to = (T + [O])[m % 4]
                parts = [(i, h) for i, (mm, h, _, _) in enumerate(SEGMENTS) if mm == m]
                for n, (i, h) in enumerate(parts):
                    last = te.matmul(to[:], vT_pad[:, i, :], wout[:, h, :], start=(n == 0),
                                     stop=(n == len(parts) - 1 and m < MC - 1))
                if m == MC - 1:
                    te.wait_ge(consts_ready, 1)
                    last = te.matmul(to[:], onehot[:], bout_row[:], start=False, stop=True)
                last.then_inc(B_done, 1)

            te.wait_ge(B_ready, MC)
            step(0, 0)
            step(0, 1)

            te.wait_ge(pT_ready, 6)
            for i, w in enumerate("krv"):
                te.wait_ge(ffn_loaded[w], 16)
                for c in range(DC):
                    n = i * DC + c
                    if n >= 3:
                        te.wait_ge(W_ready, n - 2)
                    for m in range(DC):
                        last = te.transpose(T[n % 3][:, m * P:(m + 1) * P], raw_w[w][:, m, c * P:(c + 1) * P],
                                            identity[:])
                    last.then_inc(W_turned, 1)
            te.wait_ge(W_ready, 3 * DC)
            turns(te, step)

        @block.scalar
        def _(act_e):
            def copy(dst, src):
                return nc.scalar.copy(dst, src)

            def exponentials(t, head_bank):
                h0, h1 = HEAD_BANKS[head_bank]
                act_e.wait_ge(max_ready, 3 * t + head_bank + 1)
                for h in range(h0, h1):
                    last = nc.scalar.activation(probs[:, h * J:(h + 1) * J], S[head_bank][:, (h - h0) * J:(h - h0 + 1) * J],
                                                ACT.Exp, bias=neg_max[:, h:h + 1], accum_out=row_sum[:, h:h + 1])
                return last

            def step(g, s):
                t, q, half = place(g, s)
                if is_tile(t):
                    if begun(t - 1):
                        act_e.wait_ge(attended, t)
                    for b, (c0, c1) in enumerate(PT_BANKS):
                        act_e.wait_ge(probs_turned, 3 * t + b + 1)
                        copy(pT_hi[:, c0:c1, :], T[b][:, 0:(c1 - c0) * P].rearrange("p (c k) -> p c k", k=P)
                             ).then_inc(pT_hi_ready, 1)
                if is_pair(q) and half == 0:
                    act_e.wait_ge(xk_ready, q + 1)
                    if begun(q - 1):
                        act_e.wait_ge(k_done, 2 * q)
                    copy(xk_hi[:], xk[:]).then_inc(xk_hi_ready, 1)
                    act_e.wait_ge(xr_ready, q + 1)
                    if begun(q - 1):
                        act_e.wait_ge(r_done, 2 * q)
                    copy(xr_hi[:], xr[:]).then_inc(xr_hi_ready, 1)
                if is_pair(q) and half == 1:
                    if begun(q - 1):
                        act_e.wait_ge(kv_done, 2 * q)
                    for j in range(2):
                        act_e.wait_ge(square_ready, 2 * q + j + 1)
                        copy(act_hi[:, 2 * j:2 * j + 2, :], act[:, 2 * j:2 * j + 2, :]).then_inc(act_hi_ready, 1)
                if is_tile(t + 1):
                    if begun(t):
                        act_e.wait_ge(probs_turned, 3 * t + 3)
                    else:
                        act_e.wait_ge(consts_ready, 1)
                    for b in range(3):
                        last = exponentials(t + 1, b)
                    last.then_inc(exp_done, 1)
                if is_tile(t + 2):
                    act_e.wait_ge(x_turned, t + 3)
                    if begun(t + 1):
                        act_e.wait_ge(scores_done, 3 * (t + 2))
                    copy(xT_hi[:], XB[:].rearrange("p (c k) -> p c k", k=P)).then_inc(xT_hi_ready, 1)
                if is_pair(q) and half == 0:
                    act_e.wait_ge(xr_split, q + 1)
                    for j in range(2):
                        act_e.wait_ge(k_done, 2 * q + j + 1)
                        nc.scalar.activation(act[:, 2 * j:2 * j + 2, :], T[j][:].rearrange("p (c k) -> p c k", k=2 * P),
                                             ACT.Relu).then_inc(relu_ready, 1)
                if is_pair(q):
                    act_e.wait_ge(r_done, 2 * q + half + 1)
                    if begun(q - 1):
                        act_e.wait_ge(out_ready, 2 * q - 1 + half)
                    nc.scalar.activation(gate[half][:], T[0 if half else 2][:], ACT.Tanh, scale=0.5
                                         ).then_inc(gate_ready, 1)
                if is_tile(t):
                    act_e.wait_ge(x2_turned, t + 1)
                    if half == 0 and is_pair(q):
                        act_e.wait_ge(halo_ready, q + 1)
                    copy(xn2T[:, :, 1 + half * P:1 + (half + 1) * P], XB[:].rearrange("p (c k) -> p c k", k=P)
                         ).then_inc(xn2T_ready, 1)

            for b, (h0, h1) in enumerate(HEAD_BANKS):
                act_e.wait_ge(keys_done, b + 1)
                if b == 0:
                    act_e.wait_ge(ctxT_turned, 1)
                copy(kT[:, h0:h1, :], S[b][:, 0:(h1 - h0) * J].rearrange("p (h j) -> p h j", j=J)).then_inc(kT_ready, 1)
            for h in range(0, HEADS, 2):
                act_e.wait_ge(wq_turned, h + 1)
                copy(wqT[:, h, :], (T + [O])[h % 4][:]).then_inc(wqT_even, 1)
            for c in range(DC):
                for b, (h0, h1) in enumerate(HEAD_BANKS):
                    act_e.wait_ge(A_done, 3 * c + b + 1)
                    copy(A_hi[:, c, h0 * J:h1 * J], (T if c % 2 else S)[b][:, 0:(h1 - h0) * J]).then_inc(A_hi_ready, 1)
            step(-1, 2)
            step(-1, 3)
            act_e.wait_ge(vT_pad_zeroed, 1)
            for b in (0, 2):
                act_e.wait_ge(values_done, b + 1)
                for i, (m, h, lo, hi) in enumerate(SEGMENTS):
                    if HEAD_BANKS[b][0] <= h < HEAD_BANKS[b][1]:
                        src = (h - HEAD_BANKS[b][0]) * J - h * J
                        last = copy(vT_pad[:, i, lo - m * P:hi - m * P], T[b][:, src + lo:src + hi])
                last.then_inc(vT_act, 1)
            for m in range(MC):
                act_e.wait_ge(B_done, m + 1)
                copy(B_hi[:, m, :], (T + [O])[m % 4][:]).then_inc(B_hi_ready, 1)
            step(0, 0)
            step(0, 1)
            for i, w in enumerate("krv"):
                for c in range(DC):
                    act_e.wait_ge(W_turned, i * DC + c + 1)
                    copy(WT[w][0][:, c, :], T[(i * DC + c) % 3][:]).then_inc(W_hi_ready, 1)
            turns(act_e, step)

        @block.vector
        def _(dve):
            v = nc.vector

            def low_part(dst, value, hi):
                return v.tensor_tensor(dst, value, hi.bitcast(F32), ALU.subtract)

            def mix(w, tmp, scaled, ready, q):
                dve.wait_ge(scaled, q + 1)
                for c in range(DC):
                    last = v.scalar_tensor_tensor(out=tmp[:, c, :], in0=xn2T[:, c, 1:2 * P + 1], scalar=mu[w][:, c:c + 1],
                                                  in1=tmp[:, c, :], op0=ALU.mult, op1=ALU.add)
                last.then_inc(ready, 1)

            def step(g, s):
                t, q, half = place(g, s)
                if is_tile(t):
                    for b, (c0, c1) in enumerate(PT_BANKS):
                        dve.wait_ge(pT_hi_ready, 3 * t + b + 1)
                        low_part(pT_lo[:, c0:c1, :], T[b][:, 0:(c1 - c0) * P].rearrange("p (c k) -> p c k", k=P),
                                 pT_hi[:, c0:c1, :]).then_inc(pT_ready, 1)
                if is_pair(q) and half == 0:
                    mix("k", xk, xk_scaled, xk_ready, q)
                if is_tile(t + 2):
                    slot = (s + 2) % 4
                    dve.wait_ge(x_loaded[slot], 16 * (g + 1 + (s + 2) // 4))
                    v.bn_stats(raw1[:], x_in[slot][:]).then_inc(raw1_ready, 1)
                    dve.wait_ge(raw1_ready, t + 3)
                    dve.nop(nofuse=True)
                    v.bn_aggr(stats1[:], raw1[:]).then_inc(stats1_ready, 1)
                if is_pair(q) and half == 0:
                    mix("r", xr, xr_scaled, xr_ready, q)
                    dve.wait_ge(xk_hi_ready, q + 1)
                    low_part(xk_lo[:], xk[:], xk_hi[:]).then_inc(xk_split, 1)
                if is_pair(q) and half == 1:
                    for j in range(2):
                        dve.wait_ge(act_hi_ready, 2 * q + j + 1)
                        low_part(act_lo[:, 2 * j:2 * j + 2, :], act[:, 2 * j:2 * j + 2, :],
                                 act_hi[:, 2 * j:2 * j + 2, :]).then_inc(act_split, 1)
                if is_tile(t + 2):
                    dve.wait_ge(rstd1_ready, t + 3)
                    if begun(t + 1):
                        dve.wait_ge(x_turned, t + 2)
                    v.tensor_scalar(xn[:], x_in[slot][:], stats1[:, 0:1], rstd1[:], ALU.subtract, ALU.mult
                                    ).then_inc(xn_ready, 1)
                if is_pair(q) and half == 0:
                    dve.wait_ge(xr_hi_ready, q + 1)
                    low_part(xr_lo[:], xr[:], xr_hi[:]).then_inc(xr_split, 1)
                if is_tile(t + 1):
                    for b, (h0, h1) in enumerate(HEAD_BANKS):
                        dve.wait_ge(scores_done, 3 * (t + 1) + b + 1)
                        v.tensor_reduce(neg_max[:, h0:h1], S[b][:, 0:(h1 - h0) * J].rearrange("p (h j) -> p h j", j=J),
                                        X, ALU.max, negate=True).then_inc(max_ready, 1)
                if is_tile(t):
                    dve.wait_ge(attended, t + 1)
                    if begun(t - 4):
                        dve.wait_ge(stored[s], 16 * g)
                    v.tensor_tensor(x2[s][:], O[:], x_in[s][:], ALU.add).then_inc(x2_ready, 1)
                    dve.wait_ge(x2_ready, t + 1)
                    v.bn_stats(raw2[:], x2[s][:]).then_inc(raw2_ready, 1)
                    dve.wait_ge(raw2_ready, t + 1)
                    dve.nop(nofuse=True)
                    v.bn_aggr(stats2[:], raw2[:]).then_inc(stats2_ready, 1)
                if is_tile(t + 1):
                    dve.wait_ge(exp_done, t + 2)
                    v.reciprocal(inv_sum[:], row_sum[:]).then_inc(inv_ready, 1)
                    dve.wait_ge(inv_ready, t + 2)
                    p3 = probs[:, 0:HJ].rearrange("p (h j) -> p h j", j=J)
                    v.tensor_tensor(p3, p3, inv_sum[:].unsqueeze(2).to_broadcast([P, HEADS, J]), ALU.mult
                                    ).then_inc(probs_ready, 1)
                if is_tile(t + 2):
                    dve.wait_ge(xT_hi_ready, t + 3)
                    low_part(xT_lo[:], XB[:].rearrange("p (c k) -> p c k", k=P), xT_hi[:]).then_inc(xT_ready, 1)
                if is_tile(t):
                    dve.wait_ge(rstd2_ready, t + 1)
                    if begun(t - 1):
                        dve.wait_ge(x2_turned, t)
                    v.tensor_scalar(xn2[:], x2[s][:], stats2[:, 0:1], rstd2[:], ALU.subtract, ALU.mult
                                    ).then_inc(xn2_ready, 1)
                if is_pair(q) and half == 1:
                    for j in range(2):
                        slot2 = x2[(s - 3 + j) % 4]
                        dve.wait_ge(gate_ready, 2 * q + j + 1)
                        dve.wait_ge(kv_done, 2 * q + j + 1)
                        v.scalar_tensor_tensor(out=gate[j][:], in0=gate[j][:], scalar=1.0, in1=T[1 + j][:],
                                               op0=ALU.add, op1=ALU.mult).then_inc(gated, 1)
                        dve.wait_ge(gated, 2 * q + j + 1)
                        v.scalar_tensor_tensor(out=slot2[:], in0=gate[j][:], scalar=0.5, in1=slot2[:],
                                               op0=ALU.mult, op1=ALU.add).then_inc(out_ready, 1)

            ctx_view = XB[:, 0:CC * J].rearrange("p (c j) -> p c j", j=J)
            dve.wait_ge(ctxT_turned, 1)
            v.tensor_reduce(ctx_sum[:], ctx_view, X, ALU.add).then_inc(ctx_summed, 1)
            dve.wait_ge(ctx_summed, 1)
            v.tensor_scalar(ctx_shift[:], ctx_sum[:], (1.0 - STRETCH) * SCALE / J, None, ALU.mult
                            ).then_inc(ctx_shifted, 1)
            v.tensor_copy(ctxT[:], ctx_view).then_inc(ctxT_ready, 1)
            dve.wait_ge(ctx_shifted, 1)
            for c in range(CC):
                last = v.tensor_scalar(ctxT_keys[:, c, :], ctx_view[:, c, :], STRETCH * SCALE, ctx_shift[:, c:c + 1],
                                       ALU.mult, ALU.add)
            last.then_inc(ctxT_ready, 1)
            for h in range(1, HEADS, 2):
                dve.wait_ge(wq_turned, h + 1)
                v.tensor_copy(wqT[:, h, :], (T + [O])[h % 4][:]).then_inc(wqT_odd, 1)
            for c in range(DC):
                for b, (h0, h1) in enumerate(HEAD_BANKS):
                    dve.wait_ge(A_hi_ready, 3 * c + b + 1)
                    cols = (c, slice(h0 * J, h1 * J))
                    low_part(A_lo[:, cols[0], cols[1]], (T if c % 2 else S)[b][:, 0:(h1 - h0) * J],
                             A_hi[:, cols[0], cols[1]]).then_inc(A_ready, 1)
            step(-1, 2)
            step(-1, 3)
            dve.wait_ge(vT_pad_zeroed, 1)
            dve.wait_ge(values_done, 2)
            for i, (m, h, lo, hi) in enumerate(SEGMENTS):
                if HEAD_BANKS[1][0] <= h < HEAD_BANKS[1][1]:
                    src = (h - HEAD_BANKS[1][0]) * J - h * J
                    last = v.tensor_copy(vT_pad[:, i, lo - m * P:hi - m * P], T[1][:, src + lo:src + hi])
            last.then_inc(vT_dve, 1)
            for m in range(MC):
                dve.wait_ge(B_hi_ready, m + 1)
                low_part(B_lo[:, m, :], (T + [O])[m % 4][:], B_hi[:, m, :]).then_inc(B_ready, 1)
            dve.wait_ge(mu_loaded, 32)
            for w in "kr":
                v.tensor_scalar(one_minus_mu[w][:], mu[w][:], -1.0, 1.0, ALU.mult, ALU.add).then_inc(mu_ready, 1)
            step(0, 0)
            step(0, 1)
            for i, w in enumerate("krv"):
                for c in range(DC):
                    dve.wait_ge(W_hi_ready, i * DC + c + 1)
                    low_part(WT[w][1][:, c, :], T[(i * DC + c) % 3][:], WT[w][0][:, c, :]).then_inc(W_ready, 1)
            turns(dve, step)

        @block.gpsimd
        def _(pool):
            gp = nc.gpsimd

            def inverse_root(stats, var, rstd, stats_ready, var_ready, rstd_ready, n):
                pool.wait_ge(stats_ready, n + 1)
                pool.nop(nofuse=True)
                gp.tensor_scalar(var[:], stats[:, 1:2], EPS, 1.0, ALU.add, ALU.mult).then_inc(var_ready, 1)
                pool.wait_ge(var_ready, n + 1)
                gp.tensor_tensor(rstd[:], var[:], minus_half[:], ALU.pow).then_inc(rstd_ready, 1)

            def scale_previous(w, tmp, scaled):
                for c in range(DC):
                    last = gp.tensor_scalar(tmp[:, c, :], xn2T[:, c, 0:2 * P], one_minus_mu[w][:, c:c + 1], 1.0,
                                            ALU.mult, ALU.mult)
                last.then_inc(scaled, 1)

            def step(g, s):
                t, q, half = place(g, s)
                if is_pair(q) and half == 0:
                    pool.wait_ge(xn2T_ready, 2 * q + 2)
                    if begun(q - 1):
                        pool.wait_ge(xk_split, q)
                    pool.nop(nofuse=True)
                    scale_previous("k", xk, xk_scaled)
                    if begun(q - 1):
                        pool.wait_ge(act_split, 2 * q)
                    pool.nop(nofuse=True)
                    scale_previous("r", xr, xr_scaled)
                if is_tile(t + 2):
                    inverse_root(stats1, var1, rstd1, stats1_ready, var1_ready, rstd1_ready, t + 2)
                if is_pair(q) and half == 0 and is_pair(q + 1):
                    pool.wait_ge(xr_ready, q + 1)
                    pool.nop(nofuse=True)
                    gp.tensor_copy(halo[:, :, 1:4], xn2T[:, :, 2 * P:2 * P + 1].to_broadcast([P, DC, 3])).then_inc(halo_kept, 1)
                    pool.wait_ge(halo_kept, q + 1)
                    pool.nop(nofuse=True)
                    pick = g & (GROUPS_PER_BATCH - 1) if s == 0 else 1
                    gp.tensor_copy(xn2T[:, :, 0:1], halo[:, :, bass.ds(pick, 1)]).then_inc(halo_ready, 1)
                if is_tile(t):
                    inverse_root(stats2, var2, rstd2, stats2_ready, var2_ready, rstd2_ready, t)
                if is_pair(q) and half == 0:
                    for j in range(2):
                        pool.wait_ge(relu_ready, 2 * q + j + 1)
                        a = act[:, 2 * j:2 * j + 2, :]
                        gp.tensor_tensor(a, a, a, ALU.mult).then_inc(square_ready, 1)

            gp.memset(identity[:], 0.0).then_inc(identity_zeroed, 1)
            pool.wait_ge(identity_zeroed, 1)
            gp.affine_select(out=identity[:], in_=identity[:], compare_op=ALU.not_equal, fill=1.0, base=0,
                             pattern=[[-1, P]], channel_multiplier=1).then_inc(identity_ready, 1)
            gp.memset(minus_half[:], -0.5)
            gp.memset(halo[:], 0.0)
            gp.memset(onehot[:], 0.0)
            gp.memset(probs[:, HJ:MC * P], 0.0).then_inc(ones_zeroed, 1)
            pool.wait_ge(ones_zeroed, 1)
            gp.memset(onehot[:, LAST - 1:LAST], 1.0)
            gp.memset(probs[:, HJ:HJ + 1], 1.0).then_inc(consts_ready, 1)
            gp.memset(vT_pad[:], 0.0).then_inc(vT_pad_zeroed, 1)
            step(-1, 2)
            step(-1, 3)
            pool.wait_ge(values_done, 3)
            gp.memset(xn2T[:, :, 0:1], 0.0)
            step(0, 0)
            step(0, 1)
            pool.wait_ge(mu_ready, 2)
            pool.wait_ge(W_turned, 3 * DC)
            turns(pool, step)


_INS = ["x", "ctx_768", "L0_xattn_Wq", "L0_xattn_Wk", "L0_xattn_Wv", "L0_xattn_Wout", "L0_xattn_bout",
        "L0_ffn_W_r", "L0_ffn_W_k", "L0_ffn_W_v", "L0_ffn_mu_r", "L0_ffn_mu_k"]


def kernel(**inputs):
    import numpy as _np
    import concourse.bacc as _bacc
    from concourse import mybir as _mybir
    from concourse.bass_utils import run_bass_kernel_spmd as _run

    nc = _bacc.Bacc("TRN2", target_bir_lowering=False, num_devices=1)
    arrays, args = {}, []
    for name in _INS:
        a = _np.ascontiguousarray(inputs[name])
        arrays[f"in_{name}"] = a
        args.append(nc.dram_tensor(f"in_{name}", a.shape, _mybir.dt.from_np(a.dtype), kind="ExternalInput").ap())
    shape = inputs["x"].shape
    args.append(nc.dram_tensor("out_0", shape, _mybir.dt.float32, kind="ExternalOutput").ap())
    xattn_ffn(nc, *args)
    r = _run(nc, [arrays], core_ids=[0])
    return r.results[0]["out_0"]
```

```python
from contextlib import ExitStack

import concourse.bass as bass
from concourse import mybir

F32 = mybir.dt.float32
F32R = mybir.dt.float32r
ALU = mybir.AluOpType
ACT = mybir.ActivationFunctionType
X = mybir.AxisListType.X

P = 128
HEADS = 8
STRETCH = 1.5
EPS = 1e-5
BANK = 512


def xattn_ffn(nc, x, ctx_768, Wq, Wk, Wv, Wout, bout, W_r, W_k, W_v, mu_r, mu_k, out):
    batches, seq, D = x.shape
    C = ctx_768.shape[2]
    J = ctx_768.shape[0] * ctx_768.shape[1]
    inner = Wq.shape[1]
    DH = inner // HEADS
    assert DH == P and D == 4 * P and C % P == 0 and P < J < 2 * P

    DC = D // P
    CC = C // P
    HJ = HEADS * J
    MC = -(-(HJ + 1) // P)
    LAST = HJ + 1 - (MC - 1) * P
    TILES = batches * seq // P
    GROUP = 4
    GROUPS = TILES // GROUP
    PAIRS = TILES // 2
    GROUPS_PER_BATCH = seq // P // GROUP
    HPB = BANK // J
    HEAD_BANKS = [(b, min(b + HPB, HEADS)) for b in range(0, HEADS, HPB)]
    PT_BANKS = [(c, min(c + 4, MC)) for c in range(0, MC, 4)]
    assert len(HEAD_BANKS) == 3 and len(PT_BANKS) == 3 and GROUPS_PER_BATCH == 4
    SCALE = float(DH) ** -0.5

    SEGMENTS = [(m, h, max(m * P, h * J), min((m + 1) * P, (h + 1) * J))
                for m in range(MC) for h in range(HEADS)
                if max(m * P, h * J) < min((m + 1) * P, (h + 1) * J)]

    xt = x.rearrange("b s d -> (b s) d")
    yt = out.rearrange("b s d -> (b s) d")
    ctx_rows = ctx_768.rearrange("b s d -> (b s) d")

    with ExitStack() as stack:
        base = -(-nc.sbuf_base // 64) * 64
        cursor = [base]

        def size_of(shape):
            n = 4
            for s in shape[1:]:
                n *= s
            return -(-n // 32) * 32

        def sb(name, shape, dt=F32, at=None):
            offset = cursor[0] if at is None else at
            if at is None:
                cursor[0] += size_of(shape)
            return nc.alloc_sbuf_tensor_at(name, shape, dt, offset=offset)

        A_hi = sb("A_hi", [P, DC, HJ], F32R)
        A_lo = sb("A_lo", [P, DC, HJ], F32R)
        at_B = cursor[0]
        B_hi = sb("B_hi", [P, MC, D], F32R)
        B_lo = sb("B_lo", [P, MC, D], F32R)
        at_ffn_weights = cursor[0]
        WT = {}
        for w in ("k", "r", "v"):
            WT[w] = (sb(f"W{w}T_hi", [P, DC, D], F32R), sb(f"W{w}T_lo", [P, DC, D], F32R))
        x_in = [sb(f"x_in{i}", [P, D]) for i in range(4)]
        xn = sb("xn", [P, D])
        at_xn2 = cursor[0]
        xn2 = sb("xn2", [P, D])
        xT_hi = sb("xT_hi", [P, DC, P], F32R)
        xT_lo = sb("xT_lo", [P, DC, P], F32R)
        probs = sb("probs", [P, MC * P])
        at_pT = cursor[0]
        pT_hi = sb("pT_hi", [P, MC, P], F32R)
        pT_lo = sb("pT_lo", [P, MC, P], F32R)
        at_x2 = cursor[0]
        x2 = [sb(f"x2_{i}", [P, D]) for i in range(4)]
        at_xn2T = cursor[0]
        xn2T = sb("xn2T", [P, DC, 2 * P + 1])
        at_mix = cursor[0]
        xk_hi = sb("xk_hi", [P, DC, 2 * P], F32R)
        xk_lo = sb("xk_lo", [P, DC, 2 * P], F32R)
        xr_hi = sb("xr_hi", [P, DC, 2 * P], F32R)
        xr_lo = sb("xr_lo", [P, DC, 2 * P], F32R)
        xk = sb("xk", [P, DC, P])
        xr = sb("xr", [P, DC, P])
        at_act = cursor[0]
        act_hi = sb("act_hi", [P, DC, 2 * P], F32R)
        act_lo = sb("act_lo", [P, DC, 2 * P], F32R)
        act = sb("act", [P, DC, 2 * P])
        gate = [sb(f"gate{i}", [P, D]) for i in range(2)]
        identity = sb("identity", [P, P])
        onehot = sb("onehot", [1, P])
        mu = {"k": sb("mu_k_cols", [P, DC]), "r": sb("mu_r_cols", [P, DC])}
        one_minus_mu = {"k": sb("omu_k_cols", [P, DC]), "r": sb("omu_r_cols", [P, DC])}
        minus_half = sb("minus_half", [P, 1])
        halo = sb("halo", [P, DC, 4])
        raw1 = sb("raw1", [P, 6])
        stats1 = sb("stats1", [P, 2])
        var1 = sb("var1", [P, 1])
        rstd1 = sb("rstd1", [P, 1])
        raw2 = sb("raw2", [P, 6])
        stats2 = sb("stats2", [P, 2])
        var2 = sb("var2", [P, 1])
        rstd2 = sb("rstd2", [P, 1])
        neg_max = sb("neg_max", [P, HEADS])
        row_sum = sb("row_sum", [P, HEADS])
        inv_sum = sb("inv_sum", [P, HEADS])
        ctx_sum = sb("ctx_sum", [P, CC])
        ctx_shift = sb("ctx_shift", [P, CC])

        wq = sb("wq", [P, DC, inner], at=at_ffn_weights)
        wqT = sb("wqT", [P, HEADS, D], at=at_ffn_weights + size_of([P, DC, inner]))
        at = at_B
        kT = sb("kT", [P, HEADS, J], at=at)
        at += size_of([P, HEADS, J])
        ctx0 = sb("ctx0", [P, C], at=at)
        at += size_of([P, C])
        ctx1 = sb("ctx1", [J - P, C], at=at)
        at += size_of([P, C])
        wk = sb("wk", [P, CC, inner], at=at)
        at += size_of([P, CC, inner])
        wv = sb("wv", [P, CC, inner], at=at)
        assert at + size_of([P, CC, inner]) <= at_ffn_weights
        vT_hi = sb("vT_hi", [P, len(SEGMENTS), P], F32R, at=at_pT)
        vT_lo = sb("vT_lo", [P, len(SEGMENTS), P], F32R, at=at_pT + size_of([P, len(SEGMENTS), P]))
        ctxT = sb("ctxT", [P, CC, J], at=at_xn2T)
        ctxT_keys = sb("ctxT_keys", [P, CC, J], at=at_xn2T + size_of([P, CC, J]))
        bout_row = sb("bout_row", [1, D], at=at_xn2)
        wout = sb("wout", [P, HEADS, D], at=at_mix)
        wout_lo = sb("wout_lo", [P, HEADS, D], F32R, at=at_mix)
        wout_hi = sb("wout_hi", [P, HEADS, D], F32R, at=at_mix + size_of([P, HEADS, D]))
        raw_w = {"k": sb("raw_wk", [P, DC, D], at=at_ffn_weights + 2 * size_of([P, DC, inner])),
                 "r": sb("raw_wr", [P, DC, D], at=at_act),
                 "v": sb("raw_wv", [P, DC, D], at=at_act + size_of([P, DC, D]))}

        def bank(name):
            return stack.enter_context(nc.psum_tensor(name, [P, BANK], F32))

        S = [bank(f"scores{i}") for i in range(3)]
        T = [bank(f"turn{i}") for i in range(3)]
        O = bank("attended")
        XB = bank("turned_x")

        def sem(name):
            return stack.enter_context(nc.semaphore(name))

        ctx_loaded = sem("ctx_loaded")
        wk_loaded = [sem(f"wk_loaded{i}") for i in range(3)]
        wq_loaded = [sem(f"wq_loaded{i}") for i in range(4)]
        wv_loaded, wout_loaded, mu_loaded = sem("wv_loaded"), sem("wout_loaded"), sem("mu_loaded")
        ffn_loaded = {w: sem(f"ffn_{w}_loaded") for w in "krv"}
        x_loaded = [sem(f"x_loaded{i}") for i in range(4)]
        stored = [sem(f"stored{i}") for i in range(4)]
        identity_zeroed, identity_ready = sem("identity_zeroed"), sem("identity_ready")
        consts_ready, vT_zeroed = sem("consts_ready"), sem("vT_zeroed")
        ones_zeroed, mu_ready = sem("ones_zeroed"), sem("mu_ready")
        ctxT_turned, ctx_summed, ctx_shifted, ctxT_keys_ready, ctxT_ready = (
            sem("ctxT_turned"), sem("ctx_summed"), sem("ctx_shifted"), sem("ctxT_keys_ready"), sem("ctxT_ready"))
        keys_done, kT_ready, wq_turned = sem("keys_done"), sem("kT_ready"), sem("wq_turned")
        wqT_even_ready, wqT_odd_ready = sem("wqT_even_ready"), sem("wqT_odd_ready")
        wout_hi_ready, wout_ready = sem("wout_hi_ready"), sem("wout_ready")
        A_done, A_hi_ready, A_ready = sem("A_done"), sem("A_hi_ready"), sem("A_ready")
        values_done, vT_hi_ready, vT_ready = sem("values_done"), sem("vT_hi_ready"), sem("vT_ready")
        B_done, B_hi_ready, B_ready = sem("B_done"), sem("B_hi_ready"), sem("B_ready")
        W_turned, W_hi_ready, W_ready = sem("W_turned"), sem("W_hi_ready"), sem("W_ready")
        raw1_ready, stats1_ready, var1_ready, rstd1_ready, xn_ready = (
            sem("raw1_ready"), sem("stats1_ready"), sem("var1_ready"), sem("rstd1_ready"), sem("xn_ready"))
        x_turned, xT_hi_ready, xT_ready = sem("x_turned"), sem("xT_hi_ready"), sem("xT_ready")
        scores_done = sem("scores_done")
        max_ready = sem("max_ready")
        exp_done, inv_ready, probs_ready = sem("exp_done"), sem("inv_ready"), sem("probs_ready")
        probs_turned, pT_hi_ready, pT_ready = (
            sem("probs_turned"), sem("pT_hi_ready"), sem("pT_ready"))
        attended, x2_ready = sem("attended"), sem("x2_ready")
        raw2_ready, stats2_ready, var2_ready, rstd2_ready, xn2_ready = (
            sem("raw2_ready"), sem("stats2_ready"), sem("var2_ready"), sem("rstd2_ready"), sem("xn2_ready"))
        x2_turned, xn2T_ready = sem("x2_turned"), sem("xn2T_ready")
        xk_scaled, xk_ready, xk_hi_ready, xk_split = (
            sem("xk_scaled"), sem("xk_ready"), sem("xk_hi_ready"), sem("xk_split"))
        xr_scaled, xr_ready, xr_hi_ready, xr_split = (
            sem("xr_scaled"), sem("xr_ready"), sem("xr_hi_ready"), sem("xr_split"))
        halo_kept, halo_ready = sem("halo_kept"), sem("halo_ready")
        k_done, relu_ready, square_ready, act_hi_ready, act_split = (
            sem("k_done"), sem("relu_ready"), sem("square_ready"), sem("act_hi_ready"), sem("act_split"))
        r_done, gate_ready, kv_done, gated, out_ready = (
            sem("r_done"), sem("gate_ready"), sem("kv_done"), sem("gated"), sem("out_ready"))

        def begun(n):
            return not isinstance(n, int) or n >= 0

        def is_tile(t):
            return not isinstance(t, int) or 0 <= t < TILES

        def is_pair(q):
            return not isinstance(q, int) or 0 <= q < PAIRS


        def place(g, s):
            return 4 * g + s, 2 * g + s // 2 - 1, s % 2

        def turns(eng, step):
            step(0, 2)
            step(0, 3)
            with eng.Fori(1, GROUPS - 1) as g:
                for s in range(GROUP):
                    step(g, s)
            for s in range(GROUP):
                step(GROUPS - 1, s)
            step(GROUPS, 0)
            step(GROUPS, 1)

        def x_view(bank):
            return bank[:].rearrange("p (c k) -> p c k", k=P)

        WQ_BANKS = T + [O, XB]
        A_BANKS = [S, T]
        V_BANKS = [O, XB, T[0]]
        B_BANKS = [T[1], T[2], T[0], O, XB]

        block = stack.enter_context(nc.Block())

        @block.sync
        def _(sp):
            wk_rows = Wk.rearrange("(c p) n -> p c n", p=P)
            wq_rows = Wq.rearrange("(c p) n -> p c n", p=P)

            def load_rows(dst, src, loaded):
                sp.dma_start(dst[:], src.rearrange("(c p) n -> p c n", p=P)).then_inc(loaded, 16)

            sp.dma_start(ctx0[:], ctx_rows[0:P, :]).then_inc(ctx_loaded, 16)
            sp.dma_start(ctx1[:], ctx_rows[P:J, :]).then_inc(ctx_loaded, 16)
            for b, (h0, h1) in enumerate(HEAD_BANKS):
                sp.dma_start(wk[:, :, h0 * P:h1 * P], wk_rows[:, :, h0 * P:h1 * P]).then_inc(wk_loaded[b], 16)
                if b == 0:
                    sp.dma_start(x_in[0][:], xt[0:P, :]).then_inc(x_loaded[0], 16)
            for i in range(4):
                cols = slice(2 * i * P, 2 * (i + 1) * P)
                sp.dma_start(wq[:, :, cols], wq_rows[:, :, cols]).then_inc(wq_loaded[i], 16)
            load_rows(wv, Wv, wv_loaded)
            sp.dma_start(x_in[1][:], xt[P:2 * P, :]).then_inc(x_loaded[1], 16)
            load_rows(wout, Wout, wout_loaded)
            sp.dma_start(bout_row[:], bout.rearrange("(a d) -> a d", a=1)).then_inc(wout_loaded, 16)
            with nc.allow_non_contiguous_dma(reason="two vectors of 512 as columns"):
                sp.dma_start(mu["k"][:], mu_k.rearrange("(c p) -> p c", p=P)).then_inc(mu_loaded, 16)
                sp.dma_start(mu["r"][:], mu_r.rearrange("(c p) -> p c", p=P)).then_inc(mu_loaded, 16)
            for i in (2, 3):
                sp.dma_start(x_in[i][:], xt[i * P:(i + 1) * P, :]).then_inc(x_loaded[i], 16)
            load_rows(raw_w["k"], W_k, ffn_loaded["k"])
            sp.wait_ge(B_done, MC)
            load_rows(raw_w["r"], W_r, ffn_loaded["r"])
            load_rows(raw_w["v"], W_v, ffn_loaded["v"])

            def step(g, s):
                t, q, half = place(g, s)
                if is_tile(t + 4) and is_tile(t):
                    sp.wait_ge(x2_ready, t + 1)
                    sp.dma_start(x_in[s][:], xt[bass.ds((t + 4) * P, P), :]).then_inc(x_loaded[s], 16)
                if is_pair(q) and half == 1:
                    for j in range(2):
                        slot = (s - 3 + j) % 4
                        sp.wait_ge(out_ready, 2 * q + j + 1)
                        sp.dma_start(yt[bass.ds((2 * q + j) * P, P), :], x2[slot][:]).then_inc(stored[slot], 16)

            step(0, 0)
            step(0, 1)
            turns(sp, step)
            for i in range(4):
                sp.wait_ge(stored[i], 16 * GROUPS)

        @block.tensor
        def _(te):
            def three_passes(psum, left, right, first, last):
                te.matmul(psum, left[0], right[0], start=first, stop=False)
                te.matmul(psum, left[0], right[1], start=False, stop=False)
                return te.matmul(psum, left[1], right[0], start=False, stop=last)

            def turn_chunks(bank, rows):
                for c in range(DC):
                    last = te.transpose(bank[:, c * P:(c + 1) * P], rows[:, c * P:(c + 1) * P], identity[:])
                return last

            def turn_x(t):
                te.wait_ge(xn_ready, t + 1)
                if begun(t - 3):
                    te.wait_ge(xn2T_ready, t - 2)
                turn_chunks(XB, xn).then_inc(x_turned, 1)

            def scores(t):
                te.wait_ge(xT_ready, t + 1)
                if begun(t - 1):
                    te.wait_ge(exp_done, t)
                for b, (h0, h1) in enumerate(HEAD_BANKS):
                    if isinstance(t, int) and t in (2, 3):
                        te.wait_ge(W_ready, 6 * (t - 1) - 2 + b)
                    n0, n1 = h0 * J, h1 * J
                    for c in range(DC):
                        last = three_passes(S[b][:, 0:n1 - n0], (xT_hi[:, c, :], xT_lo[:, c, :]),
                                            (A_hi[:, c, n0:n1], A_lo[:, c, n0:n1]), c == 0, c == DC - 1)
                    last.then_inc(scores_done, 1)

            def turn_probs(t, q, half):
                te.wait_ge(probs_ready, t + 1)
                for b, (c0, c1) in enumerate(PT_BANKS):
                    if half == 1 and is_pair(q):
                        if b == 0:
                            te.wait_ge(gate_ready, 2 * q + 1)
                        else:
                            te.wait_ge(relu_ready, 2 * q + b)
                    if half == 0 and begun(q - 1):
                        if b == 0:
                            te.wait_ge(gate_ready, 2 * q)
                        else:
                            te.wait_ge(gated, 2 * q + b - 2)
                    for c in range(c0, c1):
                        last = te.transpose(T[b][:, (c - c0) * P:(c - c0 + 1) * P],
                                            probs[:, c * P:(c + 1) * P], identity[:])
                    last.then_inc(probs_turned, 1)

            def turn_x2(t):
                te.wait_ge(xn2_ready, t + 1)
                if is_tile(t + 2):
                    te.wait_ge(xT_ready, t + 3)
                elif begun(t - 1):
                    te.wait_ge(xn2T_ready, t)
                turn_chunks(XB, xn2).then_inc(x2_turned, 1)

            def attend(t):
                if begun(t - 1):
                    te.wait_ge(x2_ready, t)
                for b, (c0, c1) in enumerate(PT_BANKS):
                    te.wait_ge(pT_ready, 3 * t + b + 1)
                    for c in range(c0, c1):
                        k = LAST if c == MC - 1 else P
                        last = three_passes(O[:], (pT_hi[0:k, c, :], pT_lo[0:k, c, :]),
                                            (B_hi[0:k, c, :], B_lo[0:k, c, :]), c == 0, c == MC - 1)
                last.then_inc(attended, 1)

            def ffn_rows(bank, parts, j, weights, ready=None):
                for c in range(DC):
                    if ready and c % 2 == 0:
                        te.wait_ge(ready[0], ready[1] + c // 2)
                    rows = tuple(p[:, c, j * P:(j + 1) * P] for p in parts)
                    last = three_passes(bank[:], rows, tuple(w[:, c, :] for w in weights), c == 0, c == DC - 1)
                return last

            def gate_rows(q, j, bare):
                if bare:
                    te.wait_ge(gate_ready, 2 * q + j)
                te.wait_ge(xr_split, 2 * q + j + 1)
                ffn_rows(T[0], (xr_hi, xr_lo), j, WT["r"]).then_inc(r_done, 1)

            def key_columns(q, bare):
                te.wait_ge(xk_split, 2 * q + 2)
                for j in range(2):
                    if bare:
                        te.wait_ge(gated, 2 * q + j - 1)
                    for m in (2 * j, 2 * j + 1):
                        for c in range(DC):
                            cols = tuple(w[:, c, m * P:(m + 1) * P] for w in WT["k"])
                            last = three_passes(T[1 + j][:, (m % 2) * 2 * P:(m % 2 + 1) * 2 * P], cols,
                                                (xk_hi[:, c, :], xk_lo[:, c, :]), c == 0, c == DC - 1)
                    last.then_inc(k_done, 1)

            def value_rows(q, j, bare):
                if bare:
                    te.wait_ge(relu_ready, 2 * q + j + 1)
                ffn_rows(T[1 + j], (act_hi, act_lo), j, WT["v"], (act_split, 2 * q + 1)).then_inc(kv_done, 1)

            def turn_weights(batch, banks):
                for n in range(3 * batch, 3 * batch + 3):
                    w, c = "krv"[n // DC], n % DC
                    te.wait_ge(ffn_loaded[w], 16)
                    for m in range(DC):
                        last = te.transpose(banks[n % 3][:, m * P:(m + 1) * P], raw_w[w][:, m, c * P:(c + 1) * P],
                                            identity[:])
                    last.then_inc(W_turned, 1)

            def step(g, s):
                t, q, half = place(g, s)
                if is_tile(t):
                    turn_probs(t, q, half)
                if is_tile(t - 1) and is_tile(t):
                    turn_x2(t - 1)
                if is_tile(t + 1):
                    scores(t + 1)
                if is_tile(t):
                    attend(t)
                if is_tile(t + 2):
                    turn_x(t + 2)
                if is_pair(q) and half == 0:
                    gate_rows(q, 0, not is_tile(t))
                    key_columns(q, not is_tile(t))
                if is_pair(q) and half == 1:
                    gate_rows(q, 1, not is_tile(t))
                    value_rows(q, 0, not is_tile(t))
                    if not is_tile(t + 1) and is_tile(t):
                        turn_x2(t)
                    value_rows(q, 1, not is_tile(t))

            def step_without_ffn(t):
                te.wait_ge(W_ready, 3) if t else te.wait_ge(B_ready, 8)
                turn_probs(t, -1, t)
                if t:
                    turn_x2(t - 1)
                scores(t + 1)
                te.wait_ge(pT_ready, 3 * t + 3)
                turn_weights(2 * t, T)
                te.wait_ge(B_ready, MC)
                attend(t)
                turn_x(t + 2)
                te.wait_ge(exp_done, t + 2)
                turn_weights(2 * t + 1, S)

            te.wait_ge(identity_ready, 1)
            te.wait_ge(ctx_loaded, 32)
            for c in range(CC):
                te.transpose(XB[:, c * J:c * J + P], ctx0[:, c * P:(c + 1) * P], identity[:])
                last = te.transpose(XB[:, c * J + P:(c + 1) * J], ctx1[:, c * P:(c + 1) * P],
                                    identity[0:J - P, 0:J - P])
            last.then_inc(ctxT_turned, 1)

            te.wait_ge(ctxT_keys_ready, 1)
            for b, (h0, h1) in enumerate(HEAD_BANKS):
                te.wait_ge(wk_loaded[b], 16)
                for h in range(h0, h1):
                    for c in range(CC):
                        last = te.matmul(S[b][:, (h - h0) * J:(h - h0 + 1) * J], wk[:, c, h * P:(h + 1) * P],
                                         ctxT_keys[:, c, :], start=(c == 0), stop=(c == CC - 1))
                last.then_inc(keys_done, 1)

            for h in range(HEADS):
                te.wait_ge(wq_loaded[h // 2], 16)
                if WQ_BANKS[h % len(WQ_BANKS)] is XB:
                    te.wait_ge(ctxT_ready, 1)
                if h >= len(WQ_BANKS):
                    n = h - len(WQ_BANKS)
                    te.wait_ge((wqT_even_ready, wqT_odd_ready)[n % 2], n // 2 + 1)
                for c in range(DC):
                    last = te.transpose(WQ_BANKS[h % len(WQ_BANKS)][:, c * P:(c + 1) * P],
                                        wq[:, c, h * P:(h + 1) * P], identity[:])
                last.then_inc(wq_turned, 1)

            for c in range(DC):
                if c >= 2:
                    te.wait_ge(A_ready, 3 * (c - 1))
                for b, (h0, h1) in enumerate(HEAD_BANKS):
                    if c == 0:
                        te.wait_ge(kT_ready, b + 1)
                        te.wait_ge(wqT_even_ready, (h1 + 1) // 2)
                        te.wait_ge(wqT_odd_ready, h1 // 2)
                    if c == 1 and b == 0:
                        te.wait_ge(wqT_even_ready, HEADS // 2)
                        te.wait_ge(wqT_odd_ready, HEADS // 2)
                    for h in range(h0, h1):
                        last = te.matmul(A_BANKS[c % 2][b][:, (h - h0) * J:(h - h0 + 1) * J],
                                         wqT[:, h, c * P:(c + 1) * P], kT[:, h, :], start=True, stop=True)
                    last.then_inc(A_done, 1)
                if c == 0:
                    turn_x(0)

            te.wait_ge(wv_loaded, 16)
            te.wait_ge(ctxT_ready, 1)
            for b, (h0, h1) in enumerate(HEAD_BANKS):
                if b == 1:
                    te.wait_ge(xT_ready, 1)
                if b == 2:
                    te.wait_ge(A_ready, 3 * DC - 2)
                for h in range(h0, h1):
                    for c in range(CC):
                        last = te.matmul(V_BANKS[b][:, (h - h0) * J:(h - h0 + 1) * J], wv[:, c, h * P:(h + 1) * P],
                                         ctxT[:, c, :], start=(c == 0), stop=(c == CC - 1))
                last.then_inc(values_done, 1)

            te.wait_ge(A_ready, 3 * DC)
            scores(0)
            te.wait_ge(vT_ready, 2)
            turn_x(1)

            te.wait_ge(wout_ready, 4)
            te.wait_ge(vT_ready, 3)
            for m in range(MC):
                if m == 4:
                    te.wait_ge(xT_ready, 2)
                if m >= len(B_BANKS):
                    te.wait_ge(B_ready, m - len(B_BANKS) + 1)
                to = B_BANKS[m % len(B_BANKS)]
                parts = [(i, h) for i, (mm, h, _, _) in enumerate(SEGMENTS) if mm == m]
                for n, (i, h) in enumerate(parts):
                    last = three_passes(to[:], (vT_hi[:, i, :], vT_lo[:, i, :]), (wout_hi[:, h, :], wout_lo[:, h, :]),
                                        n == 0, n == len(parts) - 1 and m < MC - 1)
                if m == MC - 1:
                    te.wait_ge(wout_loaded, 32)
                    te.wait_ge(consts_ready, 1)
                    last = te.matmul(to[:], onehot[:], bout_row[:], start=False, stop=True)
                last.then_inc(B_done, 1)

            step_without_ffn(0)
            step_without_ffn(1)
            te.wait_ge(W_ready, 9)
            turns(te, step)

        @block.scalar
        def _(act_e):
            copy = nc.scalar.copy

            def probs_hi(t):
                if begun(t - 1):
                    act_e.wait_ge(attended, t)
                for b, (c0, c1) in enumerate(PT_BANKS):
                    act_e.wait_ge(probs_turned, 3 * t + b + 1)
                    copy(pT_hi[:, c0:c1, :], T[b][:, 0:(c1 - c0) * P].rearrange("p (c k) -> p c k", k=P)
                         ).then_inc(pT_hi_ready, 1)

            def ffn_input(t, half, pair):
                act_e.wait_ge(x2_turned, t + 1)
                if begun(pair - 1):
                    act_e.wait_ge(halo_ready, pair)
                copy(xn2T[:, :, 1 + half * P:1 + (half + 1) * P], x_view(XB)).then_inc(xn2T_ready, 1)

            def mixed_hi(t, half, pair):
                cols = slice(half * P, (half + 1) * P)
                act_e.wait_ge(xk_ready, t + 1)
                if begun(pair - 1):
                    act_e.wait_ge(k_done, 2 * pair)
                copy(xk_hi[:, :, cols], xk[:]).then_inc(xk_hi_ready, 1)
                act_e.wait_ge(xr_ready, t + 1)
                if begun(pair - 1):
                    act_e.wait_ge(r_done, t - 1)
                copy(xr_hi[:, :, cols], xr[:]).then_inc(xr_hi_ready, 1)

            def squares_hi(q):
                if begun(q - 1):
                    act_e.wait_ge(kv_done, 2 * q)
                for j in range(2):
                    act_e.wait_ge(square_ready, 2 * q + j + 1)
                    copy(act_hi[:, 2 * j:2 * j + 2, :], act[:, 2 * j:2 * j + 2, :]).then_inc(act_hi_ready, 1)

            def exponentials(t):
                if begun(t - 1):
                    act_e.wait_ge(probs_turned, 3 * t)
                else:
                    act_e.wait_ge(consts_ready, 1)
                for b, (h0, h1) in enumerate(HEAD_BANKS):
                    act_e.wait_ge(max_ready, 3 * t + b + 1)
                    for h in range(h0, h1):
                        last = nc.scalar.activation(probs[:, h * J:(h + 1) * J], S[b][:, (h - h0) * J:(h - h0 + 1) * J],
                                                    ACT.Exp, bias=neg_max[:, h:h + 1], accum_out=row_sum[:, h:h + 1])
                last.then_inc(exp_done, 1)

            def x_hi(t):
                act_e.wait_ge(x_turned, t + 1)
                if begun(t - 1):
                    act_e.wait_ge(scores_done, 3 * t)
                copy(xT_hi[:], x_view(XB)).then_inc(xT_hi_ready, 1)

            def open_gate(q, half):
                act_e.wait_ge(r_done, 2 * q + half + 1)
                if begun(q - 1):
                    act_e.wait_ge(out_ready, 2 * q - 1 + half)
                nc.scalar.activation(gate[half][:], T[0][:], ACT.Tanh, scale=0.5).then_inc(gate_ready, 1)

            def rectify(q):
                if begun(q - 1):
                    act_e.wait_ge(act_split, 2 * q)
                for j in range(2):
                    act_e.wait_ge(k_done, 2 * q + j + 1)
                    nc.scalar.activation(act[:, 2 * j:2 * j + 2, :], T[1 + j][:].rearrange("p (c k) -> p c k", k=2 * P),
                                         ACT.Relu).then_inc(relu_ready, 1)

            def weights_hi(batch):
                for n in range(3 * batch, 3 * batch + 3):
                    act_e.wait_ge(W_turned, n + 1)
                    copy(WT["krv"[n // DC]][0][:, n % DC, :], (T, S)[batch % 2][n % 3][:]).then_inc(W_hi_ready, 1)

            def step(g, s):
                t, q, half = place(g, s)
                if is_tile(t):
                    probs_hi(t)
                if is_tile(t - 1):
                    ffn_input(t - 1, 1 - half, q if half == 0 else q + 1)
                if is_pair(q) and half == 1:
                    squares_hi(q)
                if is_tile(t - 1):
                    mixed_hi(t - 1, 1 - half, q if half == 0 else q + 1)
                if is_tile(t + 1):
                    exponentials(t + 1)
                if not is_pair(q):
                    weights_hi(2 * t)
                if is_tile(t + 2):
                    x_hi(t + 2)
                if not is_pair(q):
                    weights_hi(2 * t + 1)
                if is_pair(q):
                    open_gate(q, half)
                if is_pair(q) and half == 0:
                    rectify(q)

            act_e.wait_ge(ctxT_keys_ready, 1)
            copy(ctxT[:], XB[:, 0:CC * J].rearrange("p (c j) -> p c j", j=J)).then_inc(ctxT_ready, 1)
            for b, (h0, h1) in enumerate(HEAD_BANKS):
                act_e.wait_ge(keys_done, b + 1)
                copy(kT[:, h0:h1, :], S[b][:, 0:(h1 - h0) * J].rearrange("p (h j) -> p h j", j=J)
                     ).then_inc(kT_ready, 1)
            for h in range(0, HEADS, 2):
                act_e.wait_ge(wq_turned, h + 1)
                copy(wqT[:, h, :], WQ_BANKS[h % len(WQ_BANKS)][:]).then_inc(wqT_even_ready, 1)
            for c in range(DC):
                for b, (h0, h1) in enumerate(HEAD_BANKS):
                    act_e.wait_ge(A_done, 3 * c + b + 1)
                    copy(A_hi[:, c, h0 * J:h1 * J], A_BANKS[c % 2][b][:, 0:(h1 - h0) * J]).then_inc(A_hi_ready, 1)
                if c == 0:
                    x_hi(0)
            act_e.wait_ge(vT_zeroed, 1)
            for b, (h0, h1) in enumerate(HEAD_BANKS):
                act_e.wait_ge(values_done, b + 1)
                for i, (m, h, lo, hi) in enumerate(SEGMENTS):
                    if h0 <= h < h1:
                        last = copy(vT_hi[:, i, lo - m * P:hi - m * P], V_BANKS[b][:, lo - h0 * J:hi - h0 * J])
                last.then_inc(vT_hi_ready, 1)
                if b == 0:
                    act_e.wait_ge(wout_loaded, 32)
                if b < 2:
                    for i in (2 * b, 2 * b + 1):
                        copy(wout_hi[:, 2 * i:2 * i + 2, :], wout[:, 2 * i:2 * i + 2, :]).then_inc(wout_hi_ready, 1)
            x_hi(1)
            for m in range(MC):
                act_e.wait_ge(B_done, m + 1)
                copy(B_hi[:, m, :], B_BANKS[m % len(B_BANKS)][:]).then_inc(B_hi_ready, 1)
                if m == 0:
                    exponentials(0)
            step(0, 0)
            step(0, 1)
            turns(act_e, step)

        @block.vector
        def _(dve):
            v = nc.vector

            def low_part(dst, value, hi):
                return v.tensor_tensor(dst, value, hi.bitcast(F32), ALU.subtract)

            def probs_lo(t):
                for b, (c0, c1) in enumerate(PT_BANKS):
                    dve.wait_ge(pT_hi_ready, 3 * t + b + 1)
                    low_part(pT_lo[:, c0:c1, :], T[b][:, 0:(c1 - c0) * P].rearrange("p (c k) -> p c k", k=P),
                             pT_hi[:, c0:c1, :]).then_inc(pT_ready, 1)

            def mix(w, tmp, scaled, ready, t, half):
                dve.wait_ge(scaled, t + 1)
                for c in range(DC):
                    last = v.scalar_tensor_tensor(out=tmp[:, c, :], in0=xn2T[:, c, 1 + half * P:1 + (half + 1) * P],
                                                  scalar=mu[w][:, c:c + 1], in1=tmp[:, c, :], op0=ALU.mult, op1=ALU.add)
                last.then_inc(ready, 1)

            def mixed_lo(w, t, half):
                tmp, hi, lo, hi_ready, split = {"k": (xk, xk_hi, xk_lo, xk_hi_ready, xk_split),
                                                "r": (xr, xr_hi, xr_lo, xr_hi_ready, xr_split)}[w]
                cols = slice(half * P, (half + 1) * P)
                dve.wait_ge(hi_ready, t + 1)
                low_part(lo[:, :, cols], tmp[:], hi[:, :, cols]).then_inc(split, 1)

            def statistics(rows, raw, stats, raw_ready, stats_ready, t):
                v.bn_stats(raw[:], rows[:]).then_inc(raw_ready, 1)
                dve.wait_ge(raw_ready, t + 1)
                dve.nop(nofuse=True)
                v.bn_aggr(stats[:], raw[:]).then_inc(stats_ready, 1)

            def x_statistics(t, slot, loads):
                dve.wait_ge(x_loaded[slot], 16 * loads)
                statistics(x_in[slot], raw1, stats1, raw1_ready, stats1_ready, t)

            def x_norm(t, slot):
                dve.wait_ge(rstd1_ready, t + 1)
                if begun(t - 1):
                    dve.wait_ge(x_turned, t)
                v.tensor_scalar(xn[:], x_in[slot][:], stats1[:, 0:1], rstd1[:], ALU.subtract, ALU.mult
                                ).then_inc(xn_ready, 1)

            def squares_lo(q):
                for j in range(2):
                    dve.wait_ge(act_hi_ready, 2 * q + j + 1)
                    low_part(act_lo[:, 2 * j:2 * j + 2, :], act[:, 2 * j:2 * j + 2, :],
                             act_hi[:, 2 * j:2 * j + 2, :]).then_inc(act_split, 1)

            def maxima(t):
                for b, (h0, h1) in enumerate(HEAD_BANKS):
                    dve.wait_ge(scores_done, 3 * t + b + 1)
                    v.tensor_reduce(neg_max[:, h0:h1], S[b][:, 0:(h1 - h0) * J].rearrange("p (h j) -> p h j", j=J),
                                    X, ALU.max, negate=True).then_inc(max_ready, 1)

            def normalise(t):
                dve.wait_ge(exp_done, t + 1)
                v.reciprocal(inv_sum[:], row_sum[:]).then_inc(inv_ready, 1)
                dve.wait_ge(inv_ready, t + 1)
                p3 = probs[:, 0:HJ].rearrange("p (h j) -> p h j", j=J)
                v.tensor_tensor(p3, p3, inv_sum[:].unsqueeze(2).to_broadcast([P, HEADS, J]), ALU.mult
                                ).then_inc(probs_ready, 1)

            def add_x(t, g, slot):
                dve.wait_ge(attended, t + 1)
                if begun(t - 4):
                    dve.wait_ge(stored[slot], 16 * g)
                v.tensor_tensor(x2[slot][:], O[:], x_in[slot][:], ALU.add).then_inc(x2_ready, 1)
                dve.wait_ge(x2_ready, t + 1)
                statistics(x2[slot], raw2, stats2, raw2_ready, stats2_ready, t)

            def x_lo(t):
                dve.wait_ge(xT_hi_ready, t + 1)
                low_part(xT_lo[:], x_view(XB), xT_hi[:]).then_inc(xT_ready, 1)

            def x2_norm(t, slot):
                dve.wait_ge(rstd2_ready, t + 1)
                if begun(t - 1):
                    dve.wait_ge(x2_turned, t)
                v.tensor_scalar(xn2[:], x2[slot][:], stats2[:, 0:1], rstd2[:], ALU.subtract, ALU.mult
                                ).then_inc(xn2_ready, 1)

            def output(q, j, slot):
                dve.wait_ge(gate_ready, 2 * q + j + 1)
                dve.wait_ge(kv_done, 2 * q + j + 1)
                v.scalar_tensor_tensor(out=gate[j][:], in0=gate[j][:], scalar=1.0, in1=T[1 + j][:],
                                       op0=ALU.add, op1=ALU.mult).then_inc(gated, 1)
                dve.wait_ge(gated, 2 * q + j + 1)
                v.scalar_tensor_tensor(out=x2[slot][:], in0=gate[j][:], scalar=0.5, in1=x2[slot][:],
                                       op0=ALU.mult, op1=ALU.add).then_inc(out_ready, 1)

            def weights_lo(batch, chunks=range(3)):
                for n in (3 * batch + i for i in chunks):
                    hi, lo = WT["krv"[n // DC]]
                    dve.wait_ge(W_hi_ready, n + 1)
                    low_part(lo[:, n % DC, :], (T, S)[batch % 2][n % 3][:], hi[:, n % DC, :]).then_inc(W_ready, 1)

            def step(g, s):
                t, q, half = place(g, s)
                if is_tile(t):
                    probs_lo(t)
                if is_tile(t - 1):
                    mix("k", xk, xk_scaled, xk_ready, t - 1, 1 - half)
                if is_tile(t + 2):
                    x_statistics(t + 2, (s + 2) % 4, g + 1 + (s + 2) // 4)
                if is_tile(t - 1):
                    mix("r", xr, xr_scaled, xr_ready, t - 1, 1 - half)
                    mixed_lo("k", t - 1, 1 - half)
                if is_pair(q) and half == 1:
                    squares_lo(q)
                if is_tile(t + 2):
                    x_norm(t + 2, (s + 2) % 4)
                if is_tile(t - 1):
                    mixed_lo("r", t - 1, 1 - half)
                if is_tile(t + 1):
                    maxima(t + 1)
                if not is_pair(q):
                    weights_lo(2 * t)
                if is_tile(t + 1):
                    normalise(t + 1)
                if is_tile(t):
                    add_x(t, g, s)
                if is_tile(t + 2):
                    x_lo(t + 2)
                if not is_pair(q):
                    weights_lo(2 * t + 1, (0,))
                if is_tile(t):
                    x2_norm(t, s)
                if not is_pair(q):
                    weights_lo(2 * t + 1, (1, 2))
                if is_pair(q) and half == 1:
                    output(q, 0, (s - 3) % 4)
                    if is_tile(t + 1) or not is_tile(t):
                        output(q, 1, (s - 2) % 4)
                if not is_tile(t) and is_tile(t - 1):
                    output(q - 1, 1, (s - 3) % 4)

            ctx_view = XB[:, 0:CC * J].rearrange("p (c j) -> p c j", j=J)
            dve.wait_ge(ctxT_turned, 1)
            v.tensor_reduce(ctx_sum[:], ctx_view, X, ALU.add).then_inc(ctx_summed, 1)
            dve.wait_ge(ctx_summed, 1)
            v.tensor_scalar(ctx_shift[:], ctx_sum[:], (1.0 - STRETCH) * SCALE / J, None, ALU.mult
                            ).then_inc(ctx_shifted, 1)
            dve.wait_ge(ctx_shifted, 1)
            for c in range(CC):
                last = v.tensor_scalar(ctxT_keys[:, c, :], ctx_view[:, c, :], STRETCH * SCALE, ctx_shift[:, c:c + 1],
                                       ALU.mult, ALU.add)
            last.then_inc(ctxT_keys_ready, 1)
            x_statistics(0, 0, 1)
            x_norm(0, 0)
            for h in range(1, HEADS, 2):
                dve.wait_ge(wq_turned, h + 1)
                v.tensor_copy(wqT[:, h, :], WQ_BANKS[h % len(WQ_BANKS)][:]).then_inc(wqT_odd_ready, 1)
            for c in range(DC):
                for b, (h0, h1) in enumerate(HEAD_BANKS):
                    dve.wait_ge(A_hi_ready, 3 * c + b + 1)
                    low_part(A_lo[:, c, h0 * J:h1 * J], A_BANKS[c % 2][b][:, 0:(h1 - h0) * J],
                             A_hi[:, c, h0 * J:h1 * J]).then_inc(A_ready, 1)
                if c == 0:
                    x_lo(0)
            x_statistics(1, 1, 1)
            x_norm(1, 1)
            dve.wait_ge(vT_zeroed, 2)
            for b, (h0, h1) in enumerate(HEAD_BANKS):
                dve.wait_ge(vT_hi_ready, b + 1)
                for i, (m, h, lo, hi) in enumerate(SEGMENTS):
                    if h0 <= h < h1:
                        last = low_part(vT_lo[:, i, lo - m * P:hi - m * P], V_BANKS[b][:, lo - h0 * J:hi - h0 * J],
                                        vT_hi[:, i, lo - m * P:hi - m * P])
                last.then_inc(vT_ready, 1)
                if b < 2:
                    for i in (2 * b, 2 * b + 1):
                        dve.wait_ge(wout_hi_ready, i + 1)
                        low_part(wout_lo[:, 2 * i:2 * i + 2, :], wout[:, 2 * i:2 * i + 2, :],
                                 wout_hi[:, 2 * i:2 * i + 2, :]).then_inc(wout_ready, 1)
            maxima(0)
            x_lo(1)
            dve.wait_ge(mu_loaded, 32)
            for w in "kr":
                v.tensor_scalar(one_minus_mu[w][:], mu[w][:], -1.0, 1.0, ALU.mult, ALU.add).then_inc(mu_ready, 1)
            for m in range(MC):
                dve.wait_ge(B_hi_ready, m + 1)
                low_part(B_lo[:, m, :], B_BANKS[m % len(B_BANKS)][:], B_hi[:, m, :]).then_inc(B_ready, 1)
                if m == 4:
                    normalise(0)
            step(0, 0)
            step(0, 1)
            turns(dve, step)

        @block.gpsimd
        def _(pool):
            gp = nc.gpsimd

            def inverse_root(stats, var, rstd, stats_ready, var_ready, rstd_ready, n):
                pool.wait_ge(stats_ready, n + 1)
                pool.nop(nofuse=True)
                gp.tensor_scalar(var[:], stats[:, 1:2], EPS, 1.0, ALU.add, ALU.mult).then_inc(var_ready, 1)
                pool.wait_ge(var_ready, n + 1)
                gp.tensor_tensor(rstd[:], var[:], minus_half[:], ALU.pow).then_inc(rstd_ready, 1)

            def x_root(t):
                inverse_root(stats1, var1, rstd1, stats1_ready, var1_ready, rstd1_ready, t)

            def scale_previous(w, tmp, scaled, split, t, half):
                if begun(t - 1):
                    pool.wait_ge(split, t)
                pool.nop(nofuse=True)
                for c in range(DC):
                    last = gp.tensor_scalar(tmp[:, c, :], xn2T[:, c, half * P:(half + 1) * P], one_minus_mu[w][:, c:c + 1],
                                            1.0, ALU.mult, ALU.mult)
                last.then_inc(scaled, 1)

            def step(g, s):
                t, q, half = place(g, s)
                if is_tile(t - 1):
                    pool.wait_ge(xn2T_ready, t)
                    scale_previous("k", xk, xk_scaled, xk_split, t - 1, 1 - half)
                    scale_previous("r", xr, xr_scaled, xr_split, t - 1, 1 - half)
                if is_tile(t + 2):
                    x_root(t + 2)
                if is_pair(q) and half == 0 and is_pair(q + 1):
                    pool.wait_ge(xr_ready, 2 * q + 2)
                    pool.nop(nofuse=True)
                    gp.tensor_copy(halo[:, :, 1:4], xn2T[:, :, 2 * P:2 * P + 1].to_broadcast([P, DC, 3])
                                   ).then_inc(halo_kept, 1)
                    pool.wait_ge(halo_kept, q + 1)
                    pool.nop(nofuse=True)
                    pick = g & (GROUPS_PER_BATCH - 1) if s == 0 else 1
                    gp.tensor_copy(xn2T[:, :, 0:1], halo[:, :, bass.ds(pick, 1)]).then_inc(halo_ready, 1)
                if is_tile(t):
                    inverse_root(stats2, var2, rstd2, stats2_ready, var2_ready, rstd2_ready, t)
                if is_pair(q) and half == 0:
                    for j in range(2):
                        pool.wait_ge(relu_ready, 2 * q + j + 1)
                        a = act[:, 2 * j:2 * j + 2, :]
                        gp.tensor_tensor(a, a, a, ALU.mult).then_inc(square_ready, 1)

            gp.memset(identity[:], 0.0).then_inc(identity_zeroed, 1)
            pool.wait_ge(identity_zeroed, 1)
            gp.affine_select(out=identity[:], in_=identity[:], compare_op=ALU.not_equal, fill=1.0, base=0,
                             pattern=[[-1, P]], channel_multiplier=1).then_inc(identity_ready, 1)
            gp.memset(minus_half[:], -0.5)
            gp.memset(halo[:], 0.0)
            gp.memset(onehot[:], 0.0)
            gp.memset(probs[:, HJ:MC * P], 0.0).then_inc(ones_zeroed, 1)
            pool.wait_ge(ones_zeroed, 1)
            gp.memset(onehot[:, LAST - 1:LAST], 1.0)
            gp.memset(probs[:, HJ:HJ + 1], 1.0).then_inc(consts_ready, 1)
            x_root(0)
            gp.memset(vT_hi[:].bitcast(F32), 0.0).then_inc(vT_zeroed, 1)
            gp.memset(vT_lo[:].bitcast(F32), 0.0).then_inc(vT_zeroed, 1)
            x_root(1)
            pool.wait_ge(values_done, 3)
            gp.memset(xn2T[:, :, 0:1], 0.0)
            pool.wait_ge(mu_ready, 2)
            step(0, 0)
            step(0, 1)
            turns(pool, step)


_INS = ["x", "ctx_768", "L0_xattn_Wq", "L0_xattn_Wk", "L0_xattn_Wv", "L0_xattn_Wout", "L0_xattn_bout",
        "L0_ffn_W_r", "L0_ffn_W_k", "L0_ffn_W_v", "L0_ffn_mu_r", "L0_ffn_mu_k"]


def kernel(**inputs):
    import numpy as _np
    import concourse.bacc as _bacc
    from concourse import mybir as _mybir
    from concourse.bass_utils import run_bass_kernel_spmd as _run

    nc = _bacc.Bacc("TRN2", target_bir_lowering=False, num_devices=1)
    arrays, args = {}, []
    for name in _INS:
        a = _np.ascontiguousarray(inputs[name])
        arrays[f"in_{name}"] = a
        args.append(nc.dram_tensor(f"in_{name}", a.shape, _mybir.dt.from_np(a.dtype), kind="ExternalInput").ap())
    shape = inputs["x"].shape
    args.append(nc.dram_tensor("out_0", shape, _mybir.dt.float32, kind="ExternalOutput").ap())
    xattn_ffn(nc, *args)
    r = _run(nc, [arrays], core_ids=[0])
    return r.results[0]["out_0"]
```

```python
from contextlib import ExitStack

import concourse.bass as bass
from concourse import mybir

F32 = mybir.dt.float32
F32R = mybir.dt.float32r
ALU = mybir.AluOpType
ACT = mybir.ActivationFunctionType
X = mybir.AxisListType.X

P = 128
HEADS = 8
STRETCH = 1.5
EPS = 1e-5
BANK = 512


def xattn_ffn(nc, x, ctx_768, Wq, Wk, Wv, Wout, bout, W_r, W_k, W_v, mu_r, mu_k, out):
    batches, seq, D = x.shape
    C = ctx_768.shape[2]
    J = ctx_768.shape[0] * ctx_768.shape[1]
    inner = Wq.shape[1]
    DH = inner // HEADS
    assert DH == P and D == 4 * P and C % P == 0 and P < J < 2 * P

    DC = D // P
    CC = C // P
    HJ = HEADS * J
    FULL = HJ // P
    MC = FULL + 1
    TILES = batches * seq // P
    GROUP = 4
    GROUPS = TILES // GROUP
    PAIRS = TILES // 2
    GROUPS_PER_BATCH = seq // P // GROUP
    HPB = BANK // J
    HEAD_BANKS = [(b, min(b + HPB, HEADS)) for b in range(0, HEADS, HPB)]
    PT_BANKS = [(c, min(c + 4, MC)) for c in range(0, MC, 4)]
    assert len(HEAD_BANKS) == 3 and len(PT_BANKS) == 3 and GROUPS_PER_BATCH == 4
    SCALE = float(DH) ** -0.5

    RA, RB = P // 2, HJ - FULL * P - P // 2
    ONES = RA + 3 * RB
    assert RA + 2 * RB == 96 and FULL * P >= (HEADS - 1) * J

    SEGMENTS = [(m, h, [(max(0, h * J - m * P), max(m * P, h * J),
                         min((m + 1) * P, (h + 1) * J) - max(m * P, h * J))])
                for m in range(FULL) for h in range(HEADS)
                if max(m * P, h * J) < min((m + 1) * P, (h + 1) * J)]
    SEGMENTS.append((FULL, HEADS - 1, [(0, FULL * P, RA)] + [(RA + i * RB, HJ - RB, RB) for i in range(3)]))

    xt = x.rearrange("b s d -> (b s) d")
    yt = out.rearrange("b s d -> (b s) d")
    ctx_rows = ctx_768.rearrange("b s d -> (b s) d")

    with ExitStack() as stack:
        base = -(-nc.sbuf_base // 64) * 64
        cursor = [base]

        def size_of(shape):
            n = 4
            for s in shape[1:]:
                n *= s
            return -(-n // 32) * 32

        def sb(name, shape, dt=F32, at=None):
            offset = cursor[0] if at is None else at
            if at is None:
                cursor[0] += size_of(shape)
            return nc.alloc_sbuf_tensor_at(name, shape, dt, offset=offset)

        A_hi = sb("A_hi", [P, DC, HJ], F32R)
        A_lo = sb("A_lo", [P, DC, HJ], F32R)
        at_B = cursor[0]
        B_hi = sb("B_hi", [P, FULL, D], F32R)
        B_lo = sb("B_lo", [P, FULL, D], F32R)
        B_packed = sb("B_packed", [P, 2, D], F32R)
        at_ffn_weights = cursor[0]
        WT = {}
        for w in ("k", "r", "v"):
            WT[w] = (sb(f"W{w}T_hi", [P, DC, D], F32R), sb(f"W{w}T_lo", [P, DC, D], F32R))
        x_in = [sb(f"x_in{i}", [P, D]) for i in range(4)]
        normed = sb("normed", [P, D])
        at_mix_now = cursor[0]
        mix_now = sb("mix_now", [P, DC, P])
        xT_hi = sb("xT_hi", [P, DC, P], F32R)
        at_xT_lo = cursor[0]
        xT_lo = sb("xT_lo", [P, DC, P], F32R)
        xT = sb("xT", [P, DC, P], at=at_xT_lo)
        probs = sb("probs", [P, MC * P])
        at_pT = cursor[0]
        pT_hi = sb("pT_hi", [P, FULL, P], F32R)
        pT_lo = sb("pT_lo", [P, FULL, P], F32R)
        pT_packed = sb("pT_packed", [P, 2, P], F32R)
        at_x2 = cursor[0]
        x2 = [sb(f"x2_{i}", [P, D]) for i in range(4)]
        at_xn2T = cursor[0]
        xn2T = sb("xn2T", [P, DC, 2 * P + 1])
        at_mix = cursor[0]
        xk_hi = sb("xk_hi", [P, DC, 2 * P], F32R)
        xk_lo = sb("xk_lo", [P, DC, 2 * P], F32R)
        xr_hi = sb("xr_hi", [P, DC, 2 * P], F32R)
        xr_lo = sb("xr_lo", [P, DC, 2 * P], F32R)
        xk = sb("xk", [P, DC, P])
        xr = sb("xr", [P, DC, P])
        at_act = cursor[0]
        act_hi = sb("act_hi", [P, DC, 2 * P], F32R)
        act_lo = sb("act_lo", [P, DC, 2 * P], F32R)
        act = sb("act", [P, DC, 2 * P])
        gate = [sb(f"gate{i}", [P, D]) for i in range(2)]
        identity = sb("identity", [P, P])
        onehot = sb("onehot", [1, P])
        mu = {"k": sb("mu_k_cols", [P, DC]), "r": sb("mu_r_cols", [P, DC])}
        one_minus_mu = {"k": sb("omu_k_cols", [P, DC]), "r": sb("omu_r_cols", [P, DC])}
        minus_half = sb("minus_half", [P, 1])
        halo = sb("halo", [P, DC, 4])
        raw1 = sb("raw1", [P, 6])
        stats1 = sb("stats1", [P, 2])
        var1 = sb("var1", [P, 1])
        rstd1 = sb("rstd1", [P, 1])
        raw2 = sb("raw2", [P, 6])
        stats2 = sb("stats2", [P, 2])
        var2 = sb("var2", [P, 1])
        rstd2 = sb("rstd2", [P, 1])
        neg_max = sb("neg_max", [P, HEADS])
        row_sum = sb("row_sum", [P, HEADS])
        inv_sum = sb("inv_sum", [P, HEADS])
        ctx_sum = sb("ctx_sum", [P, CC])
        ctx_shift = sb("ctx_shift", [P, CC])

        wq = sb("wq", [P, DC, inner], at=at_ffn_weights)
        wqT = sb("wqT", [P, HEADS, D], at=at_ffn_weights + size_of([P, DC, inner]))
        at = at_B
        kT = sb("kT", [P, HEADS, J], at=at)
        at += size_of([P, HEADS, J])
        ctx0 = sb("ctx0", [P, C], at=at)
        at += size_of([P, C])
        ctx1 = sb("ctx1", [J - P, C], at=at)
        at += size_of([P, C])
        wk = sb("wk", [P, CC, inner], at=at)
        at += size_of([P, CC, inner])
        wv = sb("wv", [P, CC, inner], at=at)
        assert at + size_of([P, CC, inner]) <= at_ffn_weights
        vT_hi = sb("vT_hi", [P, len(SEGMENTS), P], F32R, at=at_pT)
        vT_lo = sb("vT_lo", [P, len(SEGMENTS), P], F32R, at=at_pT + size_of([P, len(SEGMENTS), P]))
        ctxT = sb("ctxT", [P, CC, J], at=at_xn2T)
        ctxT_keys = sb("ctxT_keys", [P, CC, J], at=at_xn2T + size_of([P, CC, J]))
        bout_row = sb("bout_row", [1, D], at=at_mix_now)
        wout = sb("wout", [P, HEADS, D], at=at_mix)
        wout_lo = sb("wout_lo", [P, HEADS, D], F32R, at=at_mix)
        wout_hi = sb("wout_hi", [P, HEADS, D], F32R, at=at_mix + size_of([P, HEADS, D]))
        raw_w = {"k": sb("raw_wk", [P, DC, D], at=at_ffn_weights + 2 * size_of([P, DC, inner])),
                 "r": sb("raw_wr", [P, DC, D], at=at_act),
                 "v": sb("raw_wv", [P, DC, D], at=at_act + size_of([P, DC, D]))}

        def bank(name):
            return stack.enter_context(nc.psum_tensor(name, [P, BANK], F32))

        S = [bank(f"scores{i}") for i in range(3)]
        T = [bank(f"turn{i}") for i in range(3)]
        O = bank("attended")
        XB = bank("turned_x")

        def sem(name):
            return stack.enter_context(nc.semaphore(name))

        ctx_loaded = sem("ctx_loaded")
        wk_loaded = [sem(f"wk_loaded{i}") for i in range(3)]
        wq_loaded = [sem(f"wq_loaded{i}") for i in range(4)]
        wv_loaded, wout_loaded, mu_loaded = sem("wv_loaded"), sem("wout_loaded"), sem("mu_loaded")
        ffn_loaded = {w: sem(f"ffn_{w}_loaded") for w in "krv"}
        x_loaded = [sem(f"x_loaded{i}") for i in range(4)]
        stored = [sem(f"stored{i}") for i in range(4)]
        identity_zeroed, identity_ready = sem("identity_zeroed"), sem("identity_ready")
        consts_ready, vT_zeroed = sem("consts_ready"), sem("vT_zeroed")
        onehot_zeroed, mu_ready = sem("onehot_zeroed"), sem("mu_ready")
        ctxT_turned, ctx_summed, ctx_shifted, ctxT_keys_ready, ctxT_ready = (
            sem("ctxT_turned"), sem("ctx_summed"), sem("ctx_shifted"), sem("ctxT_keys_ready"), sem("ctxT_ready"))
        keys_done, kT_ready, wq_turned = sem("keys_done"), sem("kT_ready"), sem("wq_turned")
        wqT_even_ready, wqT_odd_ready = sem("wqT_even_ready"), sem("wqT_odd_ready")
        wout_hi_ready, wout_ready = sem("wout_hi_ready"), sem("wout_ready")
        A_done, A_hi_ready, A_ready = sem("A_done"), sem("A_hi_ready"), sem("A_ready")
        values_done, vT_hi_ready, vT_ready = sem("values_done"), sem("vT_hi_ready"), sem("vT_ready")
        B_done, B_hi_ready, B_ready = sem("B_done"), sem("B_hi_ready"), sem("B_ready")
        B_packed_ready, ones_ready = sem("B_packed_ready"), sem("ones_ready")
        W_turned, W_hi_ready, W_ready = sem("W_turned"), sem("W_hi_ready"), sem("W_ready")
        raw1_ready, stats1_ready, var1_ready, rstd1_ready, xn_ready = (
            sem("raw1_ready"), sem("stats1_ready"), sem("var1_ready"), sem("rstd1_ready"), sem("xn_ready"))
        x_turned, xT_hi_ready, xT_ready = sem("x_turned"), sem("xT_hi_ready"), sem("xT_ready")
        scores_done = sem("scores_done")
        max_ready = sem("max_ready")
        exp_done, inv_ready, probs_ready = sem("exp_done"), sem("inv_ready"), sem("probs_ready")
        probs_turned, pT_hi_ready, pT_ready = (
            sem("probs_turned"), sem("pT_hi_ready"), sem("pT_ready"))
        attended, x2_ready = sem("attended"), sem("x2_ready")
        raw2_ready, stats2_ready, var2_ready, rstd2_ready, xn2_ready = (
            sem("raw2_ready"), sem("stats2_ready"), sem("var2_ready"), sem("rstd2_ready"), sem("xn2_ready"))
        xn2T_ready = sem("xn2T_ready")
        now_scaled = sem("now_scaled")
        xk_scaled, xk_ready, xk_hi_ready, xk_split = (
            sem("xk_scaled"), sem("xk_ready"), sem("xk_hi_ready"), sem("xk_split"))
        xr_scaled, xr_ready, xr_hi_ready, xr_split = (
            sem("xr_scaled"), sem("xr_ready"), sem("xr_hi_ready"), sem("xr_split"))
        halo_zeroed, halo_kept, halo_ready = sem("halo_zeroed"), sem("halo_kept"), sem("halo_ready")
        k_done, relu_ready, square_ready, act_hi_ready, act_split = (
            sem("k_done"), sem("relu_ready"), sem("square_ready"), sem("act_hi_ready"), sem("act_split"))
        r_done, gate_ready, kv_done, gated, out_ready = (
            sem("r_done"), sem("gate_ready"), sem("kv_done"), sem("gated"), sem("out_ready"))

        def begun(n):
            return not isinstance(n, int) or n >= 0

        def is_tile(t):
            return not isinstance(t, int) or 0 <= t < TILES

        def is_pair(q):
            return not isinstance(q, int) or 0 <= q < PAIRS

        def turned_by_pe(t):
            return isinstance(t, int) and t in (2, 3)


        def place(g, s):
            return 4 * g + s, 2 * g + s // 2 - 1, s % 2

        def turns(eng, step):
            step(0, 2)
            step(0, 3)
            with eng.Fori(1, GROUPS - 1) as g:
                for s in range(GROUP):
                    step(g, s)
            for s in range(GROUP):
                step(GROUPS - 1, s)
            step(GROUPS, 0)
            step(GROUPS, 1)

        def x_view(bank):
            return bank[:].rearrange("p (c k) -> p c k", k=P)

        WQ_BANKS = T + [O, XB]
        A_BANKS = [S, T]
        V_BANKS = [O, XB, T[0]]
        B_BANKS = [T[1], T[2], T[0], O, XB]

        block = stack.enter_context(nc.Block())

        @block.sync
        def _(sp):
            wk_rows = Wk.rearrange("(c p) n -> p c n", p=P)
            wq_rows = Wq.rearrange("(c p) n -> p c n", p=P)

            def load_rows(dst, src, loaded):
                sp.dma_start(dst[:], src.rearrange("(c p) n -> p c n", p=P)).then_inc(loaded, 16)

            sp.dma_start(ctx0[:], ctx_rows[0:P, :]).then_inc(ctx_loaded, 16)
            sp.dma_start(ctx1[:], ctx_rows[P:J, :]).then_inc(ctx_loaded, 16)
            for b, (h0, h1) in enumerate(HEAD_BANKS):
                sp.dma_start(wk[:, :, h0 * P:h1 * P], wk_rows[:, :, h0 * P:h1 * P]).then_inc(wk_loaded[b], 16)
                if b == 0:
                    sp.dma_start(x_in[0][:], xt[0:P, :]).then_inc(x_loaded[0], 16)
            for i in range(4):
                cols = slice(2 * i * P, 2 * (i + 1) * P)
                sp.dma_start(wq[:, :, cols], wq_rows[:, :, cols]).then_inc(wq_loaded[i], 16)
            load_rows(wv, Wv, wv_loaded)
            sp.dma_start(x_in[1][:], xt[P:2 * P, :]).then_inc(x_loaded[1], 16)
            load_rows(wout, Wout, wout_loaded)
            sp.dma_start(bout_row[:], bout.rearrange("(a d) -> a d", a=1)).then_inc(wout_loaded, 16)
            with nc.allow_non_contiguous_dma(reason="two vectors of 512 as columns"):
                sp.dma_start(mu["k"][:], mu_k.rearrange("(c p) -> p c", p=P)).then_inc(mu_loaded, 16)
                sp.dma_start(mu["r"][:], mu_r.rearrange("(c p) -> p c", p=P)).then_inc(mu_loaded, 16)
            for i in (2, 3):
                sp.dma_start(x_in[i][:], xt[i * P:(i + 1) * P, :]).then_inc(x_loaded[i], 16)
            load_rows(raw_w["k"], W_k, ffn_loaded["k"])
            sp.wait_ge(B_done, MC)
            load_rows(raw_w["r"], W_r, ffn_loaded["r"])
            load_rows(raw_w["v"], W_v, ffn_loaded["v"])

            def step(g, s):
                t, q, half = place(g, s)
                if is_tile(t + 4) and is_tile(t):
                    sp.wait_ge(x2_ready, t + 1)
                    sp.dma_start(x_in[s][:], xt[bass.ds((t + 4) * P, P), :]).then_inc(x_loaded[s], 16)
                if is_pair(q) and half == 1:
                    for j in range(2):
                        slot = (s - 3 + j) % 4
                        sp.wait_ge(out_ready, 2 * q + j + 1)
                        sp.dma_start(yt[bass.ds((2 * q + j) * P, P), :], x2[slot][:]).then_inc(stored[slot], 16)

            step(0, 0)
            step(0, 1)
            turns(sp, step)
            for i in range(4):
                sp.wait_ge(stored[i], 16 * GROUPS)

        @block.tensor
        def _(te):
            def three_passes(psum, left, right, first, last):
                te.matmul(psum, left[0], right[0], start=first, stop=False)
                te.matmul(psum, left[0], right[1], start=False, stop=False)
                return te.matmul(psum, left[1], right[0], start=False, stop=last)

            def turn_chunks(bank, rows):
                for c in range(DC):
                    last = te.transpose(bank[:, c * P:(c + 1) * P], rows[:, c * P:(c + 1) * P], identity[:])
                return last

            def scores(t):
                te.wait_ge(xT_ready, t + 1)
                if begun(t - 1):
                    te.wait_ge(exp_done, t)
                for b, (h0, h1) in enumerate(HEAD_BANKS):
                    if isinstance(t, int) and t in (2, 3):
                        te.wait_ge(W_ready, 6 * (t - 1) - 2 + b)
                    n0, n1 = h0 * J, h1 * J
                    for c in range(DC):
                        last = three_passes(S[b][:, 0:n1 - n0], (xT_hi[:, c, :], xT_lo[:, c, :]),
                                            (A_hi[:, c, n0:n1], A_lo[:, c, n0:n1]), c == 0, c == DC - 1)
                    last.then_inc(scores_done, 1)

            def turn_probs(t, q, half):
                te.wait_ge(probs_ready, t + 1)
                for b, (c0, c1) in enumerate(PT_BANKS):
                    if isinstance(t, int) and t in (1, 2):
                        te.wait_ge(W_ready, 6 * (t - 1) + b + 1)
                    if half == 1 and is_pair(q):
                        if b == 0:
                            te.wait_ge(gate_ready, 2 * q + 1)
                        else:
                            te.wait_ge(relu_ready, 2 * q + b)
                    if half == 0 and begun(q - 1):
                        if b == 0:
                            te.wait_ge(gate_ready, 2 * q)
                        else:
                            te.wait_ge(gated, 2 * q + b - 2)
                    for c in range(c0, c1):
                        last = te.transpose(T[b][:, (c - c0) * P:(c - c0 + 1) * P],
                                            probs[:, c * P:(c + 1) * P], identity[:])
                    last.then_inc(probs_turned, 1)

            def attend(t):
                if begun(t - 1):
                    te.wait_ge(x2_ready, t)
                for b, (c0, c1) in enumerate(PT_BANKS):
                    te.wait_ge(pT_ready, 3 * t + b + 1)
                    for c in range(c0, min(c1, FULL)):
                        three_passes(O[:], (pT_hi[:, c, :], pT_lo[:, c, :]), (B_hi[:, c, :], B_lo[:, c, :]),
                                     c == 0, False)
                te.matmul(O[:], pT_packed[:, 0, :], B_packed[:, 0, :], start=False, stop=False)
                last = te.matmul(O[:], pT_packed[:, 1, :], B_packed[:, 1, :], start=False, stop=True)
                last.then_inc(attended, 1)

            def ffn_rows(bank, parts, j, weights, ready=None):
                for c in range(DC):
                    if ready and c % 2 == 0:
                        te.wait_ge(ready[0], ready[1] + c // 2)
                    rows = tuple(p[:, c, j * P:(j + 1) * P] for p in parts)
                    last = three_passes(bank[:], rows, tuple(w[:, c, :] for w in weights), c == 0, c == DC - 1)
                return last

            def gate_rows(q, j, bare):
                if bare:
                    te.wait_ge(gate_ready, 2 * q + j)
                te.wait_ge(xr_split, 2 * q + j + 1)
                ffn_rows(T[0], (xr_hi, xr_lo), j, WT["r"]).then_inc(r_done, 1)

            def key_columns(q, bare):
                te.wait_ge(xk_split, 2 * q + 2)
                for j in range(2):
                    if bare:
                        te.wait_ge(gated, 2 * q + j - 1)
                    for m in (2 * j, 2 * j + 1):
                        for c in range(DC):
                            cols = tuple(w[:, c, m * P:(m + 1) * P] for w in WT["k"])
                            last = three_passes(T[1 + j][:, (m % 2) * 2 * P:(m % 2 + 1) * 2 * P], cols,
                                                (xk_hi[:, c, :], xk_lo[:, c, :]), c == 0, c == DC - 1)
                    last.then_inc(k_done, 1)

            def value_rows(q, j, bare):
                if bare:
                    te.wait_ge(relu_ready, 2 * q + j + 1)
                ffn_rows(T[1 + j], (act_hi, act_lo), j, WT["v"], (act_split, 2 * q + 1)).then_inc(kv_done, 1)

            def turn_weights(batch, banks):
                for n in range(3 * batch, 3 * batch + 3):
                    w, c = "krv"[n // DC], n % DC
                    te.wait_ge(ffn_loaded[w], 16)
                    for m in range(DC):
                        last = te.transpose(banks[n % 3][:, m * P:(m + 1) * P], raw_w[w][:, m, c * P:(c + 1) * P],
                                            identity[:])
                    last.then_inc(W_turned, 1)

            def step(g, s):
                t, q, half = place(g, s)
                if is_tile(t):
                    turn_probs(t, q, half)
                if is_tile(t + 1):
                    scores(t + 1)
                if is_tile(t):
                    attend(t)
                if is_pair(q) and half == 0:
                    gate_rows(q, 0, not is_tile(t))
                    key_columns(q, not is_tile(t))
                if is_pair(q) and half == 1:
                    gate_rows(q, 1, not is_tile(t))
                    value_rows(q, 0, not is_tile(t))
                    value_rows(q, 1, not is_tile(t))

            def step_without_ffn(t):
                if t == 0:
                    te.wait_ge(B_ready, 8)
                turn_probs(t, -1, t)
                scores(t + 1)
                te.wait_ge(pT_ready, 3 * t + 3)
                turn_weights(2 * t, T)
                te.wait_ge(B_ready, MC)
                te.wait_ge(B_packed_ready, 1)
                te.wait_ge(xn_ready, t + 3)
                if t:
                    te.wait_ge(xT_ready, 3)
                turn_chunks(XB, normed).then_inc(x_turned, 1)
                attend(t)
                te.wait_ge(exp_done, t + 2)
                turn_weights(2 * t + 1, S)

            te.wait_ge(identity_ready, 1)
            te.wait_ge(ctx_loaded, 32)
            for c in range(CC):
                te.transpose(XB[:, c * J:c * J + P], ctx0[:, c * P:(c + 1) * P], identity[:])
                last = te.transpose(XB[:, c * J + P:(c + 1) * J], ctx1[:, c * P:(c + 1) * P],
                                    identity[0:J - P, 0:J - P])
            last.then_inc(ctxT_turned, 1)

            te.wait_ge(ctxT_keys_ready, 1)
            for b, (h0, h1) in enumerate(HEAD_BANKS):
                te.wait_ge(wk_loaded[b], 16)
                for h in range(h0, h1):
                    for c in range(CC):
                        last = te.matmul(S[b][:, (h - h0) * J:(h - h0 + 1) * J], wk[:, c, h * P:(h + 1) * P],
                                         ctxT_keys[:, c, :], start=(c == 0), stop=(c == CC - 1))
                last.then_inc(keys_done, 1)

            for h in range(HEADS):
                te.wait_ge(wq_loaded[h // 2], 16)
                if WQ_BANKS[h % len(WQ_BANKS)] is XB:
                    te.wait_ge(ctxT_ready, 1)
                if h >= len(WQ_BANKS):
                    n = h - len(WQ_BANKS)
                    te.wait_ge((wqT_even_ready, wqT_odd_ready)[n % 2], n // 2 + 1)
                for c in range(DC):
                    last = te.transpose(WQ_BANKS[h % len(WQ_BANKS)][:, c * P:(c + 1) * P],
                                        wq[:, c, h * P:(h + 1) * P], identity[:])
                last.then_inc(wq_turned, 1)

            for c in range(DC):
                if c >= 2:
                    te.wait_ge(A_ready, 3 * (c - 1))
                for b, (h0, h1) in enumerate(HEAD_BANKS):
                    if c == 0:
                        te.wait_ge(kT_ready, b + 1)
                        te.wait_ge(wqT_even_ready, (h1 + 1) // 2)
                        te.wait_ge(wqT_odd_ready, h1 // 2)
                    if c == 1 and b == 0:
                        te.wait_ge(wqT_even_ready, HEADS // 2)
                        te.wait_ge(wqT_odd_ready, HEADS // 2)
                    for h in range(h0, h1):
                        last = te.matmul(A_BANKS[c % 2][b][:, (h - h0) * J:(h - h0 + 1) * J],
                                         wqT[:, h, c * P:(c + 1) * P], kT[:, h, :], start=True, stop=True)
                    last.then_inc(A_done, 1)

            te.wait_ge(wv_loaded, 16)
            te.wait_ge(ctxT_ready, 1)
            for b, (h0, h1) in enumerate(HEAD_BANKS):
                if b == 2:
                    te.wait_ge(A_ready, 3 * DC - 2)
                for h in range(h0, h1):
                    for c in range(CC):
                        last = te.matmul(V_BANKS[b][:, (h - h0) * J:(h - h0 + 1) * J], wv[:, c, h * P:(h + 1) * P],
                                         ctxT[:, c, :], start=(c == 0), stop=(c == CC - 1))
                last.then_inc(values_done, 1)

            te.wait_ge(A_ready, 3 * DC)
            scores(0)

            te.wait_ge(wout_ready, 4)
            te.wait_ge(vT_ready, 3)
            for m in range(MC):
                if m >= len(B_BANKS):
                    te.wait_ge(B_ready, m - len(B_BANKS) + 1)
                to = B_BANKS[m % len(B_BANKS)]
                parts = [(i, h) for i, (mm, h, _) in enumerate(SEGMENTS) if mm == m]
                for n, (i, h) in enumerate(parts):
                    last = three_passes(to[:], (vT_hi[:, i, :], vT_lo[:, i, :]), (wout_hi[:, h, :], wout_lo[:, h, :]),
                                        n == 0, n == len(parts) - 1 and m < MC - 1)
                if m == MC - 1:
                    te.wait_ge(wout_loaded, 32)
                    te.wait_ge(consts_ready, 1)
                    last = te.matmul(to[:], onehot[:], bout_row[:], start=False, stop=True)
                last.then_inc(B_done, 1)

            step_without_ffn(0)
            step_without_ffn(1)
            turns(te, step)

        @block.scalar
        def _(act_e):
            copy = nc.scalar.copy

            def probs_hi(t):
                if begun(t - 1):
                    act_e.wait_ge(attended, t)
                else:
                    act_e.wait_ge(ones_ready, 1)
                for b, (c0, c1) in enumerate(PT_BANKS):
                    act_e.wait_ge(probs_turned, 3 * t + b + 1)
                    full = min(c1, FULL) - c0
                    last = copy(pT_hi[:, c0:c0 + full, :], T[b][:, 0:full * P].rearrange("p (c k) -> p c k", k=P))
                    if c1 > FULL:
                        rest = T[b][:, full * P:(full + 1) * P]
                        copy(pT_packed[0:RA, 0, :], rest[0:RA, :])
                        copy(pT_packed[RA:P, 0, :], rest[0:RA, :])
                        last = copy(pT_packed[RA:ONES, 1, :], rest[RA:ONES, :])
                    last.then_inc(pT_hi_ready, 1)

            def scale_previous(t, half, pair):
                act_e.wait_ge(xn2T_ready, t + 1)
                if half == 0 and begun(pair - 1):
                    act_e.wait_ge(halo_ready, pair)
                elif half == 0:
                    act_e.wait_ge(halo_zeroed, 1)
                for w, tmp, scaled, split in (("k", xk, xk_scaled, xk_split), ("r", xr, xr_scaled, xr_split)):
                    if begun(t - 1):
                        act_e.wait_ge(split, t)
                    for c in range(DC):
                        last = nc.scalar.activation(tmp[:, c, :], xn2T[:, c, half * P:(half + 1) * P], ACT.Copy,
                                                    scale=one_minus_mu[w][:, c:c + 1])
                    last.then_inc(scaled, 1)

            def mixed_hi(w, t, half, pair):
                cols = slice(half * P, (half + 1) * P)
                tmp, hi, ready, hi_ready = {"k": (xk, xk_hi, xk_ready, xk_hi_ready),
                                            "r": (xr, xr_hi, xr_ready, xr_hi_ready)}[w]
                act_e.wait_ge(ready, t + 1)
                if begun(pair - 1):
                    act_e.wait_ge(k_done, 2 * pair) if w == "k" else act_e.wait_ge(r_done, t - 1)
                copy(hi[:, :, cols], tmp[:]).then_inc(hi_ready, 1)

            def squares_hi(q):
                if begun(q - 1):
                    act_e.wait_ge(kv_done, 2 * q)
                for j in range(2):
                    act_e.wait_ge(square_ready, 2 * q + j + 1)
                    copy(act_hi[:, 2 * j:2 * j + 2, :], act[:, 2 * j:2 * j + 2, :]).then_inc(act_hi_ready, 1)

            def exponentials(t):
                if begun(t - 1):
                    act_e.wait_ge(probs_turned, 3 * t)
                else:
                    act_e.wait_ge(consts_ready, 1)
                for b, (h0, h1) in enumerate(HEAD_BANKS):
                    act_e.wait_ge(max_ready, 3 * t + b + 1)
                    if h1 == HEADS:
                        again = S[b][:, (h1 - h0) * J - RB:(h1 - h0) * J].unsqueeze(1).to_broadcast([P, 2, RB])
                        nc.scalar.activation(probs[:, HJ:HJ + 2 * RB].rearrange("p (i j) -> p i j", j=RB), again,
                                             ACT.Exp, bias=neg_max[:, HEADS - 1:HEADS])
                    for h in range(h0, h1):
                        last = nc.scalar.activation(probs[:, h * J:(h + 1) * J], S[b][:, (h - h0) * J:(h - h0 + 1) * J],
                                                    ACT.Exp, bias=neg_max[:, h:h + 1], accum_out=row_sum[:, h:h + 1])
                last.then_inc(exp_done, 1)

            def normalise(t):
                act_e.wait_ge(inv_ready, t + 1)
                for h in range(HEADS):
                    last = nc.scalar.mul(probs[:, h * J:(h + 1) * J], probs[:, h * J:(h + 1) * J], inv_sum[:, h:h + 1])
                again = probs[:, HJ:HJ + 2 * RB]
                last = nc.scalar.mul(again, again, inv_sum[:, HEADS - 1:HEADS])
                last.then_inc(probs_ready, 1)

            def x_hi(t):
                act_e.wait_ge(x_turned, t + 1)
                if begun(t - 1):
                    act_e.wait_ge(scores_done, 3 * t)
                copy(xT_hi[:], x_view(XB) if turned_by_pe(t) else xT[:]).then_inc(xT_hi_ready, 1)

            def open_gate(q, half):
                act_e.wait_ge(r_done, 2 * q + half + 1)
                if begun(q - 1):
                    act_e.wait_ge(out_ready, 2 * q - 1 + half)
                nc.scalar.activation(gate[half][:], T[0][:], ACT.Tanh, scale=0.5).then_inc(gate_ready, 1)

            def rectify(q):
                if begun(q - 1):
                    act_e.wait_ge(act_split, 2 * q)
                for j in range(2):
                    act_e.wait_ge(k_done, 2 * q + j + 1)
                    nc.scalar.activation(act[:, 2 * j:2 * j + 2, :], T[1 + j][:].rearrange("p (c k) -> p c k", k=2 * P),
                                         ACT.Relu).then_inc(relu_ready, 1)

            def weights_hi(batch):
                for n in range(3 * batch, 3 * batch + 3):
                    act_e.wait_ge(W_turned, n + 1)
                    copy(WT["krv"[n // DC]][0][:, n % DC, :], (T, S)[batch % 2][n % 3][:]).then_inc(W_hi_ready, 1)

            def step(g, s):
                t, q, half = place(g, s)
                if is_tile(t):
                    probs_hi(t)
                if is_tile(t - 1):
                    scale_previous(t - 1, 1 - half, q if half == 0 else q + 1)
                if is_pair(q) and half == 1:
                    squares_hi(q)
                if is_tile(t - 1):
                    mixed_hi("k", t - 1, 1 - half, q if half == 0 else q + 1)
                if is_tile(t + 1):
                    exponentials(t + 1)
                if is_tile(t - 1):
                    mixed_hi("r", t - 1, 1 - half, q if half == 0 else q + 1)
                if turned_by_pe(t + 2):
                    x_hi(t + 2)
                if not is_pair(q):
                    weights_hi(2 * t)
                if is_tile(t + 1):
                    normalise(t + 1)
                if is_tile(t + 2) and not turned_by_pe(t + 2):
                    x_hi(t + 2)
                if not is_pair(q):
                    weights_hi(2 * t + 1)
                if is_pair(q):
                    open_gate(q, half)
                if is_pair(q) and half == 0:
                    rectify(q)

            act_e.wait_ge(ctxT_keys_ready, 1)
            copy(ctxT[:], XB[:, 0:CC * J].rearrange("p (c j) -> p c j", j=J)).then_inc(ctxT_ready, 1)
            for b, (h0, h1) in enumerate(HEAD_BANKS):
                act_e.wait_ge(keys_done, b + 1)
                copy(kT[:, h0:h1, :], S[b][:, 0:(h1 - h0) * J].rearrange("p (h j) -> p h j", j=J)
                     ).then_inc(kT_ready, 1)
            for h in range(0, HEADS, 2):
                act_e.wait_ge(wq_turned, h + 1)
                copy(wqT[:, h, :], WQ_BANKS[h % len(WQ_BANKS)][:]).then_inc(wqT_even_ready, 1)
            for c in range(DC):
                for b, (h0, h1) in enumerate(HEAD_BANKS):
                    act_e.wait_ge(A_done, 3 * c + b + 1)
                    copy(A_hi[:, c, h0 * J:h1 * J], A_BANKS[c % 2][b][:, 0:(h1 - h0) * J]).then_inc(A_hi_ready, 1)
                if c == 0:
                    x_hi(0)
            act_e.wait_ge(vT_zeroed, 1)
            for b, (h0, h1) in enumerate(HEAD_BANKS):
                act_e.wait_ge(values_done, b + 1)
                for i, (m, h, pieces) in enumerate(SEGMENTS):
                    if h0 <= h < h1:
                        for to, start, n in pieces:
                            last = copy(vT_hi[:, i, to:to + n], V_BANKS[b][:, start - h0 * J:start - h0 * J + n])
                last.then_inc(vT_hi_ready, 1)
                if b == 0:
                    act_e.wait_ge(wout_loaded, 32)
                if b < 2:
                    for i in (2 * b, 2 * b + 1):
                        copy(wout_hi[:, 2 * i:2 * i + 2, :], wout[:, 2 * i:2 * i + 2, :]).then_inc(wout_hi_ready, 1)
            for m in range(MC):
                act_e.wait_ge(B_done, m + 1)
                rows = B_BANKS[m % len(B_BANKS)]
                if m < FULL:
                    copy(B_hi[:, m, :], rows[:]).then_inc(B_hi_ready, 1)
                else:
                    copy(B_packed[0:RA, 0, :], rows[0:RA, :])
                    copy(B_packed[:, 1, :], rows[:]).then_inc(B_hi_ready, 1)
                    act_e.wait_ge(B_ready, MC)
                    copy(B_packed[RA:RA + RB, 1, :], rows[RA:RA + RB, :])
                    copy(B_packed[RA + 2 * RB:ONES + 1, 1, :], rows[RA + 2 * RB:ONES + 1, :]
                         ).then_inc(B_packed_ready, 1)
                if m == 0:
                    exponentials(0)
                if m == 4:
                    x_hi(1)
                if m == 5:
                    normalise(0)
            step(0, 0)
            step(0, 1)
            turns(act_e, step)

        @block.vector
        def _(dve):
            v = nc.vector

            def low_part(dst, value, hi):
                return v.tensor_tensor(dst, value, hi.bitcast(F32), ALU.subtract)

            def probs_lo(t):
                for b, (c0, c1) in enumerate(PT_BANKS):
                    dve.wait_ge(pT_hi_ready, 3 * t + b + 1)
                    full = min(c1, FULL) - c0
                    last = low_part(pT_lo[:, c0:c0 + full, :], T[b][:, 0:full * P].rearrange("p (c k) -> p c k", k=P),
                                    pT_hi[:, c0:c0 + full, :])
                    if c1 > FULL:
                        rest = T[b][:, full * P:(full + 1) * P]
                        low_part(pT_packed[0:RA, 1, :], rest[0:RA, :], pT_packed[0:RA, 0, :])
                        third = slice(RA + 2 * RB, ONES)
                        last = low_part(pT_packed[third, 1, :], rest[third, :], pT_packed[third, 1, :])
                    last.then_inc(pT_ready, 1)

            def mixed_lo(w, t, half):
                tmp, hi, lo, hi_ready, split = {"k": (xk, xk_hi, xk_lo, xk_hi_ready, xk_split),
                                                "r": (xr, xr_hi, xr_lo, xr_hi_ready, xr_split)}[w]
                cols = slice(half * P, (half + 1) * P)
                dve.wait_ge(hi_ready, t + 1)
                low_part(lo[:, :, cols], tmp[:], hi[:, :, cols]).then_inc(split, 1)

            def statistics(rows, raw, stats, raw_ready, stats_ready, t):
                v.bn_stats(raw[:], rows[:]).then_inc(raw_ready, 1)
                dve.wait_ge(raw_ready, t + 1)
                dve.nop(nofuse=True)
                v.bn_aggr(stats[:], raw[:]).then_inc(stats_ready, 1)

            def x_statistics(t, slot, loads):
                dve.wait_ge(x_loaded[slot], 16 * loads)
                statistics(x_in[slot], raw1, stats1, raw1_ready, stats1_ready, t)

            def x_norm(t, slot):
                dve.wait_ge(rstd1_ready, t + 1)
                if begun(t - 3):
                    dve.wait_ge(xn2T_ready, t - 2)
                elif begun(t - 1):
                    dve.wait_ge(x_turned, t)
                v.tensor_scalar(normed[:], x_in[slot][:], stats1[:, 0:1], rstd1[:], ALU.subtract, ALU.mult
                                ).then_inc(xn_ready, 1)

            def turn(dst, groups):
                blocks = normed[:].rearrange("p (c q k) -> p c q k", c=DC, k=32)
                for i in groups:
                    for q in range(4):
                        last = v.transpose(dst[32 * q:32 * q + 32, :, 32 * i:32 * i + 32],
                                           blocks[32 * i:32 * i + 32, :, q, :])
                return last

            def x_turn(t):
                dve.wait_ge(xn_ready, t + 1)
                if begun(t - 1):
                    dve.wait_ge(scores_done, 3 * t)
                turn(xT, range(4)).then_inc(x_turned, 1)

            def x2_turn(t, half, pair, groups):
                if 0 in groups:
                    dve.wait_ge(xn2_ready, t + 1)
                    if begun(pair - 1):
                        dve.wait_ge(halo_ready, pair)
                last = turn(xn2T[:, :, 1 + half * P:1 + (half + 1) * P], groups)
                if 3 in groups:
                    last.then_inc(xn2T_ready, 1)

            def squares_lo(q):
                for j in range(2):
                    dve.wait_ge(act_hi_ready, 2 * q + j + 1)
                    low_part(act_lo[:, 2 * j:2 * j + 2, :], act[:, 2 * j:2 * j + 2, :],
                             act_hi[:, 2 * j:2 * j + 2, :]).then_inc(act_split, 1)

            def maxima(t):
                for b, (h0, h1) in enumerate(HEAD_BANKS):
                    dve.wait_ge(scores_done, 3 * t + b + 1)
                    v.tensor_reduce(neg_max[:, h0:h1], S[b][:, 0:(h1 - h0) * J].rearrange("p (h j) -> p h j", j=J),
                                    X, ALU.max, negate=True).then_inc(max_ready, 1)

            def inverse_sums(t):
                dve.wait_ge(exp_done, t + 1)
                v.reciprocal(inv_sum[:], row_sum[:]).then_inc(inv_ready, 1)

            def add_x(t, g, slot):
                dve.wait_ge(attended, t + 1)
                if begun(t - 4):
                    dve.wait_ge(stored[slot], 16 * g)
                v.tensor_tensor(x2[slot][:], O[:], x_in[slot][:], ALU.add).then_inc(x2_ready, 1)
                dve.wait_ge(x2_ready, t + 1)
                statistics(x2[slot], raw2, stats2, raw2_ready, stats2_ready, t)

            def x_lo(t):
                dve.wait_ge(xT_hi_ready, t + 1)
                low_part(xT_lo[:], x_view(XB) if turned_by_pe(t) else xT[:], xT_hi[:]).then_inc(xT_ready, 1)

            def x2_norm(t, slot):
                dve.wait_ge(rstd2_ready, t + 1)
                if is_tile(t + 2):
                    dve.wait_ge(x_turned, t + 3)
                else:
                    dve.wait_ge(xn2T_ready, t)
                v.tensor_scalar(normed[:], x2[slot][:], stats2[:, 0:1], rstd2[:], ALU.subtract, ALU.mult
                                ).then_inc(xn2_ready, 1)

            def output(q, j, slot):
                dve.wait_ge(gate_ready, 2 * q + j + 1)
                dve.wait_ge(kv_done, 2 * q + j + 1)
                v.scalar_tensor_tensor(out=gate[j][:], in0=gate[j][:], scalar=1.0, in1=T[1 + j][:],
                                       op0=ALU.add, op1=ALU.mult).then_inc(gated, 1)
                dve.wait_ge(gated, 2 * q + j + 1)
                v.scalar_tensor_tensor(out=x2[slot][:], in0=gate[j][:], scalar=0.5, in1=x2[slot][:],
                                       op0=ALU.mult, op1=ALU.add).then_inc(out_ready, 1)

            def weights_lo(batch, chunks):
                for n in (3 * batch + i for i in chunks):
                    hi, lo = WT["krv"[n // DC]]
                    dve.wait_ge(W_hi_ready, n + 1)
                    low_part(lo[:, n % DC, :], (T, S)[batch % 2][n % 3][:], hi[:, n % DC, :]).then_inc(W_ready, 1)

            def step(g, s):
                t, q, half = place(g, s)
                if is_tile(t):
                    probs_lo(t)
                if is_tile(t + 2):
                    x_statistics(t + 2, (s + 2) % 4, g + 1 + (s + 2) // 4)
                if is_tile(t - 1):
                    mixed_lo("k", t - 1, 1 - half)
                if is_pair(q) and half == 1:
                    squares_lo(q)
                if is_tile(t + 2):
                    x_norm(t + 2, (s + 2) % 4)
                if is_tile(t + 1):
                    maxima(t + 1)
                if is_tile(t + 2) and not turned_by_pe(t + 2):
                    x_turn(t + 2)
                if is_tile(t + 1):
                    inverse_sums(t + 1)
                if is_tile(t - 1):
                    mixed_lo("r", t - 1, 1 - half)
                if turned_by_pe(t + 2):
                    x_lo(t + 2)
                if not is_pair(q):
                    weights_lo(2 * t, (0, 1, 2))
                if is_tile(t):
                    add_x(t, g, s)
                if not is_pair(q):
                    weights_lo(2 * t + 1, (0,))
                if is_tile(t + 2) and not turned_by_pe(t + 2):
                    x_lo(t + 2)
                if is_tile(t):
                    x2_norm(t, s)
                if not is_pair(q):
                    weights_lo(2 * t + 1, (1, 2))
                last = is_tile(t) and not is_tile(t + 1)
                if is_tile(t) and (half == 0 or last):
                    x2_turn(t, half, q + 1, range(4))
                if is_pair(q) and half == 1:
                    output(q, 0, (s - 3) % 4)
                    if is_tile(t) and not last:
                        x2_turn(t, half, q + 1, range(1))
                    output(q, 1, (s - 2) % 4)
                if is_tile(t) and half == 1 and not last:
                    x2_turn(t, half, q + 1, range(1, 4) if is_pair(q) else range(4))

            ctx_view = XB[:, 0:CC * J].rearrange("p (c j) -> p c j", j=J)
            dve.wait_ge(ctxT_turned, 1)
            v.tensor_reduce(ctx_sum[:], ctx_view, X, ALU.add).then_inc(ctx_summed, 1)
            dve.wait_ge(ctx_summed, 1)
            v.tensor_scalar(ctx_shift[:], ctx_sum[:], (1.0 - STRETCH) * SCALE / J, None, ALU.mult
                            ).then_inc(ctx_shifted, 1)
            dve.wait_ge(ctx_shifted, 1)
            for c in range(CC):
                last = v.tensor_scalar(ctxT_keys[:, c, :], ctx_view[:, c, :], STRETCH * SCALE, ctx_shift[:, c:c + 1],
                                       ALU.mult, ALU.add)
            last.then_inc(ctxT_keys_ready, 1)
            x_statistics(0, 0, 1)
            x_norm(0, 0)
            x_turn(0)
            for h in range(1, HEADS, 2):
                dve.wait_ge(wq_turned, h + 1)
                v.tensor_copy(wqT[:, h, :], WQ_BANKS[h % len(WQ_BANKS)][:]).then_inc(wqT_odd_ready, 1)
            for c in range(DC):
                for b, (h0, h1) in enumerate(HEAD_BANKS):
                    dve.wait_ge(A_hi_ready, 3 * c + b + 1)
                    low_part(A_lo[:, c, h0 * J:h1 * J], A_BANKS[c % 2][b][:, 0:(h1 - h0) * J],
                             A_hi[:, c, h0 * J:h1 * J]).then_inc(A_ready, 1)
                if c == 0:
                    x_lo(0)
            x_statistics(1, 1, 1)
            x_norm(1, 1)
            dve.wait_ge(vT_zeroed, 2)
            for b, (h0, h1) in enumerate(HEAD_BANKS):
                dve.wait_ge(vT_hi_ready, b + 1)
                for i, (m, h, pieces) in enumerate(SEGMENTS):
                    if h0 <= h < h1:
                        for to, start, n in pieces:
                            last = low_part(vT_lo[:, i, to:to + n], V_BANKS[b][:, start - h0 * J:start - h0 * J + n],
                                            vT_hi[:, i, to:to + n])
                last.then_inc(vT_ready, 1)
                if b < 2:
                    for i in (2 * b, 2 * b + 1):
                        dve.wait_ge(wout_hi_ready, i + 1)
                        low_part(wout_lo[:, 2 * i:2 * i + 2, :], wout[:, 2 * i:2 * i + 2, :],
                                 wout_hi[:, 2 * i:2 * i + 2, :]).then_inc(wout_ready, 1)
            maxima(0)
            dve.wait_ge(mu_loaded, 32)
            for w in "kr":
                v.tensor_scalar(one_minus_mu[w][:], mu[w][:], -1.0, 1.0, ALU.mult, ALU.add).then_inc(mu_ready, 1)
            for m in range(MC):
                dve.wait_ge(B_hi_ready, m + 1)
                rows = B_BANKS[m % len(B_BANKS)]
                if m < FULL:
                    low_part(B_lo[:, m, :], rows[:], B_hi[:, m, :]).then_inc(B_ready, 1)
                else:
                    low_part(B_packed[RA:P, 0, :], rows[0:RA, :], B_packed[0:RA, 1, :])
                    low_part(B_packed[RA:P, 1, :], rows[RA:P, :], B_packed[RA:P, 1, :]).then_inc(B_ready, 1)
                    v.memset(pT_packed[RA + 2 * RB:P, 1, :].bitcast(F32), 1.0).then_inc(ones_ready, 1)
                if m == 0:
                    x_turn(1)
                    inverse_sums(0)
                if m == 6:
                    x_lo(1)
            step(0, 0)
            step(0, 1)
            turns(dve, step)

        @block.gpsimd
        def _(pool):
            gp = nc.gpsimd

            def inverse_root(stats, var, rstd, stats_ready, var_ready, rstd_ready, n):
                pool.wait_ge(stats_ready, n + 1)
                pool.nop(nofuse=True)
                gp.tensor_scalar(var[:], stats[:, 1:2], EPS, 1.0, ALU.add, ALU.mult).then_inc(var_ready, 1)
                pool.wait_ge(var_ready, n + 1)
                gp.tensor_tensor(rstd[:], var[:], minus_half[:], ALU.pow).then_inc(rstd_ready, 1)

            def x_root(t):
                inverse_root(stats1, var1, rstd1, stats1_ready, var1_ready, rstd1_ready, t)

            def mix(w, t, half):
                tmp, scaled, ready, number = {"k": (xk, xk_scaled, xk_ready, 1), "r": (xr, xr_scaled, xr_ready, 2)}[w]
                if w == "r":
                    pool.wait_ge(xk_ready, t + 1)
                else:
                    pool.wait_ge(xn2T_ready, t + 1)
                    if begun(t - 1):
                        pool.wait_ge(xr_ready, t)
                pool.nop(nofuse=True)
                for c in range(DC):
                    last = gp.tensor_scalar(mix_now[:, c, :], xn2T[:, c, 1 + half * P:1 + (half + 1) * P],
                                            mu[w][:, c:c + 1], 1.0, ALU.mult, ALU.mult)
                last.then_inc(now_scaled, 1)
                pool.wait_ge(now_scaled, 2 * t + number)
                pool.wait_ge(scaled, t + 1)
                gp.tensor_tensor(tmp[:], mix_now[:], tmp[:], ALU.add).then_inc(ready, 1)

            def step(g, s):
                t, q, half = place(g, s)
                if is_tile(t - 1):
                    mix("k", t - 1, 1 - half)
                if is_tile(t + 2):
                    x_root(t + 2)
                if is_tile(t - 1):
                    mix("r", t - 1, 1 - half)
                if is_pair(q) and half == 0 and is_pair(q + 1):
                    pool.wait_ge(xr_ready, 2 * q + 2)
                    pool.nop(nofuse=True)
                    gp.tensor_copy(halo[:, :, 1:4], xn2T[:, :, 2 * P:2 * P + 1].to_broadcast([P, DC, 3])
                                   ).then_inc(halo_kept, 1)
                    pool.wait_ge(halo_kept, q + 1)
                    pool.nop(nofuse=True)
                    pick = g & (GROUPS_PER_BATCH - 1) if s == 0 else 1
                    gp.tensor_copy(xn2T[:, :, 0:1], halo[:, :, bass.ds(pick, 1)]).then_inc(halo_ready, 1)
                if is_tile(t):
                    inverse_root(stats2, var2, rstd2, stats2_ready, var2_ready, rstd2_ready, t)
                if is_pair(q) and half == 0:
                    for j in range(2):
                        pool.wait_ge(relu_ready, 2 * q + j + 1)
                        a = act[:, 2 * j:2 * j + 2, :]
                        gp.tensor_tensor(a, a, a, ALU.mult).then_inc(square_ready, 1)

            gp.memset(identity[:], 0.0).then_inc(identity_zeroed, 1)
            pool.wait_ge(identity_zeroed, 1)
            gp.affine_select(out=identity[:], in_=identity[:], compare_op=ALU.not_equal, fill=1.0, base=0,
                             pattern=[[-1, P]], channel_multiplier=1).then_inc(identity_ready, 1)
            gp.memset(minus_half[:], -0.5)
            gp.memset(halo[:], 0.0)
            gp.memset(onehot[:], 0.0)
            gp.memset(probs[:, HJ + 2 * RB:MC * P], 0.0).then_inc(onehot_zeroed, 1)
            pool.wait_ge(onehot_zeroed, 1)
            gp.memset(onehot[:, ONES:ONES + 2], 1.0).then_inc(consts_ready, 1)
            x_root(0)
            gp.memset(vT_hi[:].bitcast(F32), 0.0).then_inc(vT_zeroed, 1)
            gp.memset(vT_lo[:].bitcast(F32), 0.0).then_inc(vT_zeroed, 1)
            x_root(1)
            pool.wait_ge(values_done, 3)
            gp.memset(xn2T[:, :, 0:1], 0.0).then_inc(halo_zeroed, 1)
            pool.wait_ge(mu_ready, 2)
            step(0, 0)
            step(0, 1)
            turns(pool, step)


_INS = ["x", "ctx_768", "L0_xattn_Wq", "L0_xattn_Wk", "L0_xattn_Wv", "L0_xattn_Wout", "L0_xattn_bout",
        "L0_ffn_W_r", "L0_ffn_W_k", "L0_ffn_W_v", "L0_ffn_mu_r", "L0_ffn_mu_k"]


def kernel(**inputs):
    import numpy as _np
    import concourse.bacc as _bacc
    from concourse import mybir as _mybir
    from concourse.bass_utils import run_bass_kernel_spmd as _run

    nc = _bacc.Bacc("TRN2", target_bir_lowering=False, num_devices=1)
    arrays, args = {}, []
    for name in _INS:
        a = _np.ascontiguousarray(inputs[name])
        arrays[f"in_{name}"] = a
        args.append(nc.dram_tensor(f"in_{name}", a.shape, _mybir.dt.from_np(a.dtype), kind="ExternalInput").ap())
    shape = inputs["x"].shape
    args.append(nc.dram_tensor("out_0", shape, _mybir.dt.float32, kind="ExternalOutput").ap())
    xattn_ffn(nc, *args)
    r = _run(nc, [arrays], core_ids=[0])
    return r.results[0]["out_0"]
```
